# Optimizing a Trainium2 kernel written in Bass

```python
import numpy as np
import jax
import jax.numpy as jnp

def _softmax(x, axis=-1):
    return jax.nn.softmax(x, axis=axis)

def _gelu(x):
    return jax.nn.gelu(x, approximate=True)

def _silu(x):
    return jax.nn.silu(x)

def _sigmoid(x):
    return jax.nn.sigmoid(x)

def _layernorm(x, axis=-1, eps=1e-05):
    m = jnp.mean(x, axis=axis, keepdims=True)
    v = jnp.var(x, axis=axis, keepdims=True)
    return (x - m) / jnp.sqrt(v + eps)

def _scatter_add(tgt, idx, src, axis=0):
    return tgt.at[idx].add(src)

def _segment_sum(src, seg, n):
    return jax.ops.segment_sum(src, seg, n)
kernel_name = 'mk_seq_preln_d1_jaxref_r8_7f64cf'

def setup_inputs(seed: int=0):
    np.random.seed(seed)
    _w = jnp.asarray

    def _L0_attn_setup():
        import jax, jax.numpy as jnp
        import numpy as np
        B, S, D, H = (2, 256, 256, 16)
        HD = D // H

        def _alibi_slopes(num_heads):
            ratio = 2.0 ** (-8.0 / num_heads)
            return ratio ** jnp.arange(1, num_heads + 1, dtype=jnp.float32)
        key = jax.random.key(seed)
        ks = jax.random.split(key, 9)
        sd = 1.0 / np.sqrt(D)
        inp = {'x': jax.random.normal(ks[0], (B, S, D), dtype=jnp.float32)}
        for i, name in enumerate(['Wq', 'Wk', 'Wv', 'Wo']):
            inp[name] = jax.random.normal(ks[1 + i], (D, D), dtype=jnp.float32) * sd
        for i, name in enumerate(['bq', 'bk', 'bv', 'bo']):
            inp[name] = jax.random.normal(ks[5 + i], (D,), dtype=jnp.float32) * 0.02
        return inp
    _L0_attn_in = _L0_attn_setup()

    def _L0_ffn_setup():
        import jax, jax.numpy as jnp
        import numpy as np
        EPS = 1e-08

        def _quantize(w):
            gamma = jnp.mean(jnp.abs(w))
            return jnp.clip(jnp.round(w / (gamma + EPS)), -1.0, 1.0)

        def _bitlinear(x, w):
            return jnp.matmul(x, _quantize(w).T)
        key = jax.random.key(seed)
        k1, k2, k3, k4 = jax.random.split(key, 4)
        d, h = (256, 704)
        x = jax.random.normal(k1, (4, 256, d), dtype=jnp.float32)
        w1 = jax.random.normal(k2, (h, d), dtype=jnp.float32)
        w2 = jax.random.normal(k3, (h, d), dtype=jnp.float32)
        w3 = jax.random.normal(k4, (d, h), dtype=jnp.float32)
        return {'x': x, 'w1': w1, 'w2': w2, 'w3': w3}
    _L0_ffn_in = _L0_ffn_setup()
    _d = {'L0_attn_x': _L0_attn_in['x'], 'L0_attn_Wq': _L0_attn_in['Wq'], 'L0_attn_bq': _L0_attn_in['bq'], 'L0_attn_Wk': _L0_attn_in['Wk'], 'L0_attn_bk': _L0_attn_in['bk'], 'L0_attn_Wv': _L0_attn_in['Wv'], 'L0_attn_bv': _L0_attn_in['bv'], 'L0_attn_Wo': _L0_attn_in['Wo'], 'L0_attn_bo': _L0_attn_in['bo'], 'L0_ffn_w1': _L0_ffn_in['w1'], 'L0_ffn_w2': _L0_ffn_in['w2'], 'L0_ffn_w3': _L0_ffn_in['w3']}
    _x0 = _d['L0_attn_x']
    _d['L0_attn_x'] = jax.random.normal(jax.random.fold_in(jax.random.key(seed), 1), (1, 2048, 256), dtype=_x0.dtype)
    del _x0
    return _d

def reference(L0_attn_x, L0_attn_Wq, L0_attn_bq, L0_attn_Wk, L0_attn_bk, L0_attn_Wv, L0_attn_bv, L0_attn_Wo, L0_attn_bo, L0_ffn_w1, L0_ffn_w2, L0_ffn_w3):

    def _L0_attn_ref(x, Wq, bq, Wk, bk, Wv, bv, Wo, bo):
        import jax, jax.numpy as jnp
        import numpy as np
        B, S, D, H = (2, 256, 256, 16)
        HD = D // H

        def _alibi_slopes(num_heads):
            ratio = 2.0 ** (-8.0 / num_heads)
            return ratio ** jnp.arange(1, num_heads + 1, dtype=jnp.float32)
        b, s, d = x.shape

        def proj(W, bias):
            return (x @ W + bias).reshape(b, s, H, HD).transpose(0, 2, 1, 3)
        q, k, v = (proj(Wq, bq), proj(Wk, bk), proj(Wv, bv))
        scores = jnp.einsum('bhqd,bhkd->bhqk', q, k) / jnp.sqrt(jnp.float32(HD))
        distances = jnp.arange(1 - s, 1, dtype=jnp.float32)
        bias = _alibi_slopes(H)[None, :, None, None] * distances[None, None, None, :]
        scores = scores + bias
        causal = jnp.tril(jnp.ones((s, s), dtype=bool))[None, None]
        scores = jnp.where(causal, scores, jnp.finfo(scores.dtype).min)
        attn = jax.nn.softmax(scores, axis=-1)
        ctx = jnp.einsum('bhqk,bhkd->bhqd', attn, v)
        ctx = ctx.transpose(0, 2, 1, 3).reshape(b, s, d)
        return ctx @ Wo + bo

    def _L0_ffn_ref(x, w1, w2, w3):
        import jax, jax.numpy as jnp
        import numpy as np
        EPS = 1e-08

        def _quantize(w):
            gamma = jnp.mean(jnp.abs(w))
            return jnp.clip(jnp.round(w / (gamma + EPS)), -1.0, 1.0)

        def _bitlinear(x, w):
            return jnp.matmul(x, _quantize(w).T)
        x1 = _bitlinear(x, w1)
        x2 = _bitlinear(x, w2)
        hidden = jax.nn.sigmoid(x1) * x2
        return _bitlinear(hidden, w3)
    x = L0_attn_x
    x = x + _L0_attn_ref(_layernorm(x, axis=-1), L0_attn_Wq, L0_attn_bq, L0_attn_Wk, L0_attn_bk, L0_attn_Wv, L0_attn_bv, L0_attn_Wo, L0_attn_bo)
    x = x + _L0_ffn_ref(_layernorm(x, axis=-1), L0_ffn_w1, L0_ffn_w2, L0_ffn_w3)
    return x

_drawn_inputs = setup_inputs


def setup_inputs(seed=0):
    import zlib

    import numpy as np

    out = dict(_drawn_inputs(seed))
    spreads = {}
    factors = {'L0_attn_bq': 6.572, 'L0_attn_bk': 8.0}
    for name, (base, spread) in spreads.items():
        noise = np.random.default_rng([zlib.crc32(name.encode()), seed]).standard_normal(out[name].shape)
        drawn = base * np.exp(spread * noise) if base else spread * noise
        out[name] = jnp.asarray(drawn.astype(out[name].dtype))
    for name, factor in factors.items():
        out[name] = (out[name] * factor).astype(out[name].dtype)
    return out
```

```python
import concourse.bass as bass
from concourse import mybir
from contextlib import ExitStack



def preln_layer(nc, x, Wq, bq, Wk, bk, Wv, bv, Wo, bo, w1, w2, w3, alibi, out):
    F32, F32R, BF16 = mybir.dt.float32, mybir.dt.float32r, mybir.dt.bfloat16
    ALU = mybir.AluOpType
    ACT = mybir.ActivationFunctionType
    AX = mybir.AxisListType

    _, T, D = x.shape
    FH = w1.shape[0]
    H = 16
    HD = D // H
    P = 128
    CH = 512
    NCH = T // CH
    TPC = CH // P
    G = 4
    NHG = H // G
    KT = D // P
    FT = (FH + P - 1) // P
    FROWS = [min(P, FH - i * P) for i in range(FT)]
    HALF = CH // 2
    EPS = 1e-5
    QEPS = 1e-8
    NEG = -3.0e38
    VW = HD + 1
    R_ALIBI = 4 * HD
    R_MAX = 96
    R_END = R_MAX + 2
    KSLOTS, QSLOTS, PSLOTS = 8, 3, 3

    units = [(c, hg) for c in range(NCH) for hg in range(NHG)]
    NU = len(units)
    n_steps = [TPC * (c + 1) for c, _ in units]
    first_step = [sum(n_steps[:u]) for u in range(NU + 1)]
    NS = first_step[NU]
    phase0 = [first_step[c * NHG] for c in range(NCH)] + [NS]
    steps = [(u, j) for u in range(NU) for j in range(n_steps[u])]

    piece0 = [sum(units[v][0] + 1 for v in range(u)) for u in range(NU + 1)]
    pieces = [(u, i) for u in range(NU) for i in range(units[u][0] + 1)]

    def max_ops(u):
        return G * TPC * (units[u][0] + 1)

    max0 = [sum(max_ops(v) + 1 for v in range(u)) for u in range(NU + 1)]

    def max_op(u, k):
        return k // (G * TPC), k // TPC % G, k % TPC

    def spare(u):
        return 2 if n_steps[u] > TPC else 1

    def max_share(u, j):
        if u + 1 >= NU:
            return range(0)
        n, m = max_ops(u + 1), n_steps[u] - spare(u)
        return range(n * min(j, m) // m, n * min(j + 1, m) // m)

    def pre_groups(c):
        return ([("xT", c, k) for k in range(KT)] + [("k", c, m) for m in range(KT)]
                + [("q", c, m) for m in range(KT)] + [("v", c, i) for i in range(TPC // 2)])

    weight_groups = [("w", i, k) for i in range(3) for k in range(2)]

    def post_groups(c):
        up = [[("up", c, h, m) for m in range(FT)] for h in range(2)]
        return ([("wo", c, 0), ("wo", c, 1), None, None, ("x2T", c, 0)] + up[0]
                + [("x2T", c, 1), ("down", c, 0), up[1][0], ("back", c, 0)] + up[1][1:]
                + [None, ("down", c, 1), None, ("back", c, 1)])

    side = [None] * NS
    for c in range(NCH):
        lst = pre_groups(c + 1) if c + 1 < NCH else [None] * len(pre_groups(0))
        lst = lst + (weight_groups if c == 0 else post_groups(c - 1))
        for i, g in enumerate(lst):
            side[phase0[c] + i] = g
    head_groups = pre_groups(0) + [("gamma",)]
    tail_groups = [g for g in post_groups(NCH - 1) if g]
    order = head_groups + [g for g in side if g] + tail_groups
    number = {g: i for i, g in enumerate(order)}
    READS_LAST = {"gamma": "v", "xT": "a", "k": "a", "q": "a", "v": "v", "w": "v", "wo": "v",
                  "x2T": "v", "up": "v", "down": "a", "back": "v"}
    NHEAD, NTAIL0 = len(head_groups), len(order) - len(tail_groups)
    bank_of, prev_user, emptied = [], [], []
    last = {}
    for i, g in enumerate(order):
        b = i % 5 if i < NHEAD else (i - NTAIL0) % 5 if i >= NTAIL0 else 0
        bank_of.append(b)
        prev_user.append(last.get(b))
        last[b] = i
        e = READS_LAST[g[0]]
        emptied.append((e, 1 + sum(READS_LAST[q[0]] == e for q in order[:i])))
    LN_AT = {0: 10, 1: 20, 2: -9, 3: -9}
    splits = [g for g in order if g[0] in "kq"]
    split_no = {g: i for i, g in enumerate(splits)}
    halves = [g for g in order if g[0] in ("x2T", "up")]
    half_no = {g: i for i, g in enumerate(halves)}
    ups = [g for g in order if g[0] == "up"]
    up_no = {g: i for i, g in enumerate(ups)}

    parts = nc.dram_tensor("parts", (2, 2, D, T), F32, kind="Internal").ap()
    alibi_parts = nc.dram_tensor("alibi_parts", (2, H, T), F32, kind="Internal").ap()
    ctx_dram = nc.dram_tensor("ctx_dram", (NCH, NHG, G, 32, CH), F32, kind="Internal").ap()

    es = ExitStack()
    with es:
        def sb(name, shape, dt=F32):
            return es.enter_context(nc.sbuf_tensor(name, shape, dt))

        def sem(name):
            return es.enter_context(nc.semaphore(name))

        kst = sb("kst", [P, KSLOTS, G, CH], F32R)
        qst = sb("qst", [P, QSLOTS, G, CH], F32R)
        probs = sb("probs", [P, PSLOTS, 2, CH])
        vals = sb("vals", [P, T // P, H, VW])
        xin = sb("xin", [P, TPC, D])
        xnT = sb("xnT", [P, KT, CH])
        wq_s, wk_s, wv_s, wo_s = (sb(n, [P, KT, D]) for n in ("wq_s", "wk_s", "wv_s", "wo_s"))
        w1T, w2T = sb("w1T", [P, KT, FH], F32R), sb("w2T", [P, KT, FH], F32R)
        w3T = sb("w3T", [P, FT, D], F32R)
        qk_f = sb("qk_f", [P, CH])
        qk_hl = sb("qk_hl", [P, 2, 2, CH])
        ctx_raw = sb("ctx_raw", [P, CH])
        work = sb("work", [P, 5120])
        ctx_c = work[:, 0:1024].rearrange("p (m n) -> p m n", m=KT)
        den_c = work[:, 1024:2048].rearrange("p (m n) -> p m n", m=KT)
        xn2 = work[:, 1024:2048].rearrange("p (t n) -> p t n", t=TPC)
        x1 = work[:, 2048:3072].rearrange("p (t n) -> p t n", t=TPC)
        th = work[:, 3072:3584].rearrange("p (i n) -> p i n", i=2)
        hid = work[:, 3584:4096].rearrange("p (i n) -> p i n", i=2)
        yT = work[:, 4096:4608].rearrange("p (m n) -> p m n", m=KT)
        fin = work[:, 4608:5120].rearrange("p (t n) -> p t n", t=2)
        w_rows = [probs[:, :, :, :].rearrange("p a b n -> p (a b n)")[:, 0:FT * D].rearrange("p (t n) -> p t n", n=D),
                  probs[:, :, :, :].rearrange("p a b n -> p (a b n)")[:, FT * D:2 * FT * D].rearrange("p (t n) -> p t n", n=D),
                  work[:, 0:KT * FH].rearrange("p (t n) -> p t n", n=FH)]
        al = work[:, 5120 - 3 * H * T // P:5120].rearrange("p (a n) -> p a n", a=3)
        tern0 = KT * FH
        tern = [work[:, tern0 + i * FT * D // 2:tern0 + (i + 1) * FT * D // 2].bitcast(BF16) for i in range(2)]
        tern.append(work[:, tern0 + FT * D:tern0 + FT * D + KT * FH // 2].bitcast(BF16))
        tern_v = [tern[0].rearrange("p (t n) -> p t n", n=D), tern[1].rearrange("p (t n) -> p t n", n=D),
                  tern[2].rearrange("p (t n) -> p t n", n=FH)]
        x2T = sb("x2T", [P, 2, KT, HALF], F32R)
        hT = sb("hT", [P, 2, FT, HALF], F32R)
        mask = sb("mask", [P, CH])
        maskb = sb("maskb", [P, P], BF16)
        ident = sb("ident", [P, P])
        identb = sb("identb", [P, P], BF16)
        ones = sb("ones", [P, P])
        bias_q, bias_k = sb("bias_q", [P, KT]), sb("bias_k", [P, KT])
        bv_b, bo_b = sb("bv_b", [P, D]), sb("bo_b", [P, D])
        bq_raw = sb("bq_raw", [P, KT])
        wsum = sb("wsum", [P, 4])
        thr = sb("thr", [P, 2, 4])
        st = sb("st", [P, TPC, 6])
        mv = sb("mv", [P, TPC, 2])
        ve = sb("ve", [P, TPC])
        mhalf = sb("mhalf", [P, TPC])
        rstd = sb("rstd", [P, TPC])
        pm = sb("pm", [P, 2, G * TPC, NCH])
        nm = sb("nm", [P, G * TPC])
        mT = sb("mT", [G * TPC, 2, P])

        pS = es.enter_context(nc.psum_tensor("pS", [P, G, CH], F32))
        pO = es.enter_context(nc.psum_tensor("pO", [P, CH], F32))
        pM = es.enter_context(nc.psum_tensor("pM", [P, 2, CH], F32))
        pW = es.enter_context(nc.psum_tensor("pW", [P, CH], F32))

        def bank(g):
            b = bank_of[number[g]]
            return pW[:, :] if b == 0 else pS[:, b - 1, :]

        x_in = sem("x_in")
        w_in = sem("w_in")
        raw_in = sem("raw_in")
        al_in = sem("al_in")
        al_out = sem("al_out")
        x1_in = sem("x1_in")
        const_ok = sem("const_ok")
        pad_ok = sem("pad_ok")
        rows_ok = sem("rows_ok")
        vself = sem("vself")
        pself = sem("pself")
        var_ok = sem("var_ok")
        rstd_ok = sem("rstd_ok")
        xn_ok = sem("xn_ok")
        xn2_ok = sem("xn2_ok")
        wsum_ok = sem("wsum_ok")
        tern_ok = sem("tern_ok")
        side_ready = sem("side_ready")
        side_a = sem("side_a")
        side_v = sem("side_v")
        half_a = sem("half_a")
        split_ok = sem("split_ok")
        parts_out = [sem(f"parts_out{i}") for i in range(2)]
        k_in = [sem(f"k_in{i}") for i in range(KSLOTS)]
        q_in = [sem(f"q_in{i}") for i in range(QSLOTS)]
        m_in = sem("m_in")
        max_ready = sem("max_ready")
        max_free = sem("max_free")
        nm_ok = sem("nm_ok")
        mT_ok = sem("mT_ok")
        scores_ready = sem("scores_ready")
        probs_ready = sem("probs_ready")
        pv_done = sem("pv_done")
        ctx_saved = sem("ctx_saved")
        ctx_out = sem("ctx_out")
        ctx_in = sem("ctx_in")
        ctx_ok = sem("ctx_ok")
        xb_ok = sem("xb_ok")
        hid_ok = sem("hid_ok")
        lo_ok = sem("lo_ok")
        out_done = sem("out_done")

        block = es.enter_context(nc.Block())

        def diag(u, j):
            return max(0, j - TPC * units[u][0]) * P

        def is_diag(u, j):
            return j >= TPC * units[u][0]

        def turns_before(u):
            return max0[u] - u

        def need_max_bank(eng, u, k):
            m = max0[u] + k - 2
            if m < 0:
                return
            v = u if k >= 2 else u - 1
            kk = m - max0[v]
            if kk == max_ops(v):
                eng.wait_ge(mT_ok, v + 1)
            else:
                eng.wait_ge(max_free, turns_before(v) + kk + 1)

        def need_side(eng, g):
            eng.wait_ge(side_ready, number[g] + 1)

        def need_empty(eng, g):
            e, n = emptied[number[g]]
            eng.wait_ge(side_a if e == "a" else side_v, n)

        @block.sync
        def _(sp):
            def load_x(c):
                if c >= 1:
                    need_side(sp, ("xT", c - 1, KT - 1))
                sp.dma_start(xin[:, :, :], x[0, c * CH:(c + 1) * CH, :].rearrange("(t p) d -> p t d", p=P))\
                    .then_inc(x_in, 16)

            def load_x1(c):
                if c >= 1:
                    need_empty(sp, ("back", c - 1, 1))
                else:
                    need_side(sp, weight_groups[-1])
                sp.dma_start(x1, x[0, c * CH:(c + 1) * CH, :].rearrange("(t p) d -> p t d", p=P))\
                    .then_inc(x1_in, 16)

            def store_parts(g):
                i = split_no[g]
                w = 0 if g[0] == "q" else 1
                sp.wait_ge(split_ok, i + 1)
                for part in range(2):
                    sp.dma_start(parts[w, part, g[2] * P:(g[2] + 1) * P, g[1] * CH:(g[1] + 1) * CH],
                                 qk_hl[:, i % 2, part, :]).then_inc(parts_out[i % 2], 16)

            def parts_there(c):
                for i in range(2):
                    n = sum(split_no[g] % 2 == i for g in splits if g[1] <= c)
                    sp.wait_ge(parts_out[i], 32 * n)

            def load_k(n):
                v, i = pieces[n]
                parts_there(i)
                if n >= KSLOTS:
                    pu, pi = pieces[n - KSLOTS]
                    sp.wait_ge(scores_ready, 2 * (first_step[pu] + TPC * pi + TPC))
                h0 = units[v][1] * G
                for b in range(4):
                    sp.dma_start(kst[b * HD:(b + 1) * HD, n % KSLOTS, :, :].bitcast(F32),
                                 parts[1, b // 2, h0 * HD:(h0 + G) * HD, i * CH:(i + 1) * CH]
                                 .rearrange("(h d) n -> d h n", h=G)).then_inc(k_in[n % KSLOTS], 16)
                sp.dma_start(kst[R_ALIBI:R_ALIBI + 2, n % KSLOTS, :, :].bitcast(F32),
                             alibi_parts[:, h0:h0 + G, i * CH:(i + 1) * CH]).then_inc(k_in[n % KSLOTS], 16)

            def load_q(v):
                c, hg = units[v]
                parts_there(c)
                if v >= QSLOTS:
                    sp.wait_ge(scores_ready, 2 * first_step[v - QSLOTS + 1])
                h0 = hg * G
                for b in range(4):
                    sp.dma_start(qst[b * HD:(b + 1) * HD, v % QSLOTS, :, :].bitcast(F32),
                                 parts[0, b % 2, h0 * HD:(h0 + G) * HD, c * CH:(c + 1) * CH]
                                 .rearrange("(h d) n -> d h n", h=G)).then_inc(q_in[v % QSLOTS], 16)

            def load_m(v):
                sp.wait_ge(mT_ok, v + 1)
                for part in range(2):
                    sp.dma_start(qst[R_MAX + part:R_MAX + part + 1, v % QSLOTS, :, :].bitcast(F32)
                                 .rearrange("o h (t n) -> o (h t) n", n=P),
                                 mT[:, part, :]).then_inc(m_in, 16)

            def store_ctx(u):
                sp.wait_ge(ctx_saved, u + 1)
                c, hg = units[u]
                sp.dma_start(ctx_dram[c, hg, :, :, :].rearrange("h r n -> (h r) n"), ctx_raw[:, :])\
                    .then_inc(ctx_out, 16)

            def load_ctx(c):
                sp.wait_ge(ctx_out, 16 * NHG * (c + 1))
                need_side(sp, ("x2T", c - 1, 1) if c >= 1 else weight_groups[-1])
                for m in range(KT):
                    for i in range(2):
                        src = ctx_dram[c, 2 * m + i, :, :, :]
                        for h in range(G):
                            r = (i * G + h) * HD
                            sp.dma_start(ctx_c[r:r + HD, m, :], src[h, 0:HD, :]).then_inc(ctx_in, 16)
                            sp.dma_start(den_c[r:r + HD, m, :],
                                         src[h, HD:HD + 1, :].to_broadcast([HD, CH]))\
                                .then_inc(ctx_in, 16)

            def store_out(c, h):
                need_empty(sp, ("back", c, h))
                t0 = c * CH + h * HALF
                sp.dma_start(out[0, t0:t0 + HALF, :].rearrange("(t p) d -> p t d", p=P), fin)\
                    .then_inc(out_done, 16)

            load_x(0)
            sp.dma_start(al[:, 0, :], alibi).then_inc(al_in, 16)
            for dst, src in ((wk_s, Wk), (wq_s, Wq), (wv_s, Wv), (wo_s, Wo)):
                sp.dma_start(dst[:, :, :], src.rearrange("(k p) n -> p k n", p=P)).then_inc(w_in, 16)
            for dst, src in ((bq_raw, bq), (bias_k, bk)):
                sp.dma_start(dst[:, :], src.rearrange("(m p) -> p m", p=P), allow_slow_non_contiguous=True)\
                    .then_inc(w_in, 16)
            for dst, src in ((bv_b, bv), (bo_b, bo)):
                sp.dma_start(dst[:, :], src.rearrange("(a n) -> a n", a=1).to_broadcast([P, D]))\
                    .then_inc(w_in, 16)
            sp.wait_ge(pad_ok, 1)
            FF = (FT - 1) * P
            for i, w in enumerate((w1, w2)):
                sp.dma_start(w_rows[i][:, 0:FT - 1, :], w[0:FF, :].rearrange("(t p) n -> p t n", p=P))\
                    .then_inc(raw_in, 16)
                sp.dma_start(w_rows[i][0:FH - FF, FT - 1, :], w[FF:FH, :]).then_inc(raw_in, 16)
            sp.dma_start(w_rows[2], w3.rearrange("(t p) n -> p t n", p=P)).then_inc(raw_in, 16)
            sp.wait_ge(vself, 2)
            for part in range(2):
                sp.dma_start(alibi_parts[part, :, :].rearrange("h (i n) -> (h i) n", n=H * T // P),
                             al[:, 1 + part, :]).then_inc(al_out, 16)
            load_x(1)
            for g in pre_groups(0):
                if g[0] in "kq":
                    store_parts(g)
            sp.wait_ge(rows_ok, 2)
            sp.wait_ge(al_out, 32)
            for n in range(2):
                load_k(n)
                load_q(n)
            load_m(0)

            k_at, q_at = {}, {}
            for n in range(2, len(pieces)):
                v, i = pieces[n]
                c = units[v][0]
                s = 0
                if n >= KSLOTS:
                    pu, pi = pieces[n - KSLOTS]
                    s = first_step[pu] + TPC * pi + TPC - 1
                if c >= 1:
                    s = max(s, phase0[c - 1] + 10)
                k_at.setdefault(s, []).append(n)
            for v in range(2, NU):
                c = units[v][0]
                s = first_step[v - QSLOTS + 1] - 1 if v >= QSLOTS else 0
                if c >= 1:
                    s = max(s, phase0[c - 1] + 10)
                q_at.setdefault(s, []).append(v)
            for s, (u, j) in enumerate(steps):
                c, hg = units[u]
                ph = s - phase0[c]
                g = side[s - 1] if s else None
                if g and g[0] in "kq":
                    store_parts(g)
                if g and g[0] == "back":
                    store_out(g[1], g[2])
                for n in k_at.get(s, []):
                    load_k(n)
                for v in q_at.get(s, []):
                    load_q(v)
                if j == n_steps[u] - spare(u) and u + 1 < NU:
                    load_m(u + 1)
                if j == 0 and u >= 1:
                    store_ctx(u - 1)
                if ph == 1 and c >= 1:
                    load_ctx(c - 1)
                    load_x1(c - 1)
                if ph == 3 and c + 2 < NCH:
                    load_x(c + 2)
            store_ctx(NU - 1)
            load_ctx(NCH - 1)
            load_x1(NCH - 1)
            for h in range(2):
                store_out(NCH - 1, h)
            sp.wait_ge(out_done, 16 * 2 * NCH)

        @block.gpsimd
        def _(pool):
            chain = [0]

            def link(ins):
                chain[0] += 1
                ins.then_inc(pself, 1)
                pool.wait_ge(pself, chain[0])

            link(nc.gpsimd.memset(mhalf[:, :], -0.5))
            for i in range(2):
                ins = nc.gpsimd.memset(w_rows[i][FROWS[FT - 1]:P, FT - 1, :], 0.0)
            ins.then_inc(pad_ok, 1)
            pool.wait_ge(pad_ok, 1)
            link(nc.gpsimd.memset(ident[:, :], 0.0))
            link(nc.gpsimd.affine_select(out=ident[:, :], in_=ident[:, :], compare_op=ALU.not_equal, fill=1.0,
                                         base=0, pattern=[[-1, P]], channel_multiplier=1))
            link(nc.gpsimd.tensor_copy(identb[:, :], ident[:, :]))
            link(nc.gpsimd.memset(mask[:, :], 0.0))
            link(nc.gpsimd.affine_select(out=mask[:, CH - P:CH], in_=mask[:, CH - P:CH], compare_op=ALU.is_ge,
                                         fill=NEG, base=0, pattern=[[-1, P]], channel_multiplier=1))
            link(nc.gpsimd.memset(maskb[:, :], 0.0))
            link(nc.gpsimd.affine_select(out=maskb[:, :], in_=maskb[:, :], compare_op=ALU.is_ge, fill=NEG,
                                         base=0, pattern=[[1, P]], channel_multiplier=-1))
            nc.gpsimd.memset(ones[:, :], 1.0).then_inc(const_ok, 1)

            pool.wait_ge(const_ok, 1)

            def power(n):
                pool.wait_ge(var_ok, n)
                nc.gpsimd.tensor_tensor(rstd[:, :], ve[:, :], mhalf[:, :], ALU.pow).then_inc(rstd_ok, 1)
                pool.wait_ge(rstd_ok, n)

            def add_bo(c):
                pool.wait_ge(x1_in, 16 * (c + 1))
                for t in range(TPC):
                    ins = nc.gpsimd.tensor_tensor(x1[:, t, :], x1[:, t, :], bo_b[:, :], ALU.add)
                    ins.then_inc(xb_ok, 1)
                    pool.wait_ge(xb_ok, TPC * c + t + 1)

            def lo_part(g):
                i, m, rows = up_no[g], g[3], FROWS[g[3]]
                pool.wait_ge(hid_ok, i + 1)
                nc.gpsimd.tensor_tensor(hT[0:rows, 1, m, :], hid[0:rows, i % 2, :],
                                        hT[0:rows, 0, m, :].bitcast(F32), ALU.subtract).then_inc(lo_ok, 1)
                pool.wait_ge(lo_ok, i + 1)

            power(1)
            power(2)
            powers = 2
            pool.wait_ge(w_in, 128)
            for s, (u, j) in enumerate(steps):
                c = units[u][0]
                ph = s - phase0[c]
                g = side[s - 1] if s else None
                if g and g[0] == "up":
                    lo_part(g)
                if ph == 2 and c >= 1:
                    add_bo(c - 1)
                if (ph == 11 and c >= 1) or (ph == LN_AT[c] + 1):
                    powers += 1
                    power(powers)
            add_bo(NCH - 1)
            power(powers + 1)
            for g in tail_groups:
                if g[0] == "up":
                    lo_part(g)

        @block.scalar
        def _(act):
            def side_op(g):
                kind = g[0]
                if kind == "xT":
                    need_side(act, g)
                    if g[1] >= 1:
                        need_side(act, ("v", g[1] - 1, 1))
                    nc.scalar.activation(xnT[:, g[2], :], bank(g), ACT.Copy).then_inc(side_a, 1)
                elif kind in "kq":
                    need_side(act, g)
                    if split_no[g] >= 1:
                        act.wait_ge(split_ok, split_no[g])
                    b, sc = (bias_k, 1.0) if kind == "k" else (bias_q, HD ** -0.5)
                    nc.scalar.activation(qk_f[:, :], bank(g), ACT.Identity, bias=b[:, g[2]:g[2] + 1],
                                         scale=sc).then_inc(side_a, 1)
                elif kind == "x2T":
                    need_side(act, g)
                    if g[2] == 1 or g[1] >= 1:
                        need_side(act, ("up", g[1] - 1 + g[2], 1 - g[2], FT - 1))
                    nc.scalar.activation(x2T[:, 0, :, :], bank(g).rearrange("p (k n) -> p k n", k=KT), ACT.Copy)\
                        .then_inc(half_a, 1)
                elif kind == "up":
                    i, rows = up_no[g], FROWS[g[3]]
                    need_side(act, g)
                    if i >= 2:
                        act.wait_ge(hid_ok, i - 1)
                    nc.scalar.activation(th[0:rows, i % 2, :], bank(g)[0:rows, 0:HALF], ACT.Tanh, scale=0.5)\
                        .then_inc(half_a, 1)
                elif kind == "down":
                    need_side(act, g)
                    if g[2] == 1 or g[1] >= 1:
                        need_side(act, ("back", g[1] - 1 + g[2], 1 - g[2]))
                    nc.scalar.activation(yT, bank(g).rearrange("p (m n) -> p m n", m=KT), ACT.Copy, scale=0.5)\
                        .then_inc(side_a, 1)

            def exps(s, p):
                u, j = steps[s]
                n = 2 * s + p
                q0 = diag(u, j)
                act.wait_ge(scores_ready, n + 1)
                if n >= PSLOTS:
                    act.wait_ge(pv_done, (n - PSLOTS) // 2 + 1)
                if n == 0:
                    act.wait_ge(tern_ok, 3)
                nc.scalar.activation(probs[:, n % PSLOTS, :, q0:CH], pS[:, 2 * p:2 * p + 2, q0:CH], ACT.Exp)\
                    .then_inc(probs_ready, 1)

            def save_ctx(u):
                act.wait_ge(pv_done, first_step[u + 1])
                if u >= 1:
                    act.wait_ge(ctx_out, 16 * u)
                nc.scalar.activation(ctx_raw[:, :], pO[:, :], ACT.Copy).then_inc(ctx_saved, 1)

            act.wait_ge(w_in, 128)
            nc.scalar.mul(bias_q[:, :], bq_raw[:, :], HD ** -0.5).then_inc(wsum_ok, 1)
            act.wait_ge(wsum_ok, 1)
            for g in head_groups:
                if g[0] in ("xT", "k", "q"):
                    side_op(g)
            act.wait_ge(raw_in, 80)
            for i in range(3):
                wr = w_rows[i].rearrange("p t n -> p (t n)")
                nc.scalar.activation(tern[i], wr, ACT.Abs, accum_out=wsum[:, i:i + 1])\
                    .then_inc(wsum_ok, 1)
            for s, (u, j) in enumerate(steps):
                exps(s, 0)
                if s and side[s - 1]:
                    side_op(side[s - 1])
                exps(s, 1)
                if j == 0 and u >= 1:
                    save_ctx(u - 1)
            save_ctx(NU - 1)
            for g in tail_groups:
                side_op(g)

        @block.tensor
        def _(pe):
            def side_group(g):
                kind = g[0]
                if prev_user[number[g]] is not None:
                    need_empty(pe, order[prev_user[number[g]]])
                w = bank(g)
                if kind == "xT":
                    pe.wait_ge(xn_ok, g[1] + 1)
                    for t in range(TPC):
                        ins = pe.transpose(w[:, t * P:(t + 1) * P], xin[:, t, g[2] * P:(g[2] + 1) * P], ident[:, :])
                elif kind in "kq":
                    need_empty(pe, ("xT", g[1], KT - 1))
                    for k in range(KT):
                        ins = pe.matmul(w, (wk_s if kind == "k" else wq_s)[:, k, g[2] * P:(g[2] + 1) * P],
                                        xnT[:, k, :], start=k == 0, stop=k == KT - 1)
                elif kind == "v":
                    for i in range(2):
                        t = 2 * g[2] + i
                        for k in range(KT):
                            ins = pe.matmul(w[:, i * D:(i + 1) * D], xnT[:, k, t * P:(t + 1) * P], wv_s[:, k, :],
                                            start=k == 0, stop=k == KT - 1)
                elif kind == "gamma":
                    pe.wait_ge(wsum_ok, 4)
                    ins = pe.matmul(w[:, 0:3], ones[:, :], wsum[:, 0:3], start=True, stop=True)
                elif kind == "w":
                    wb = w.bitcast(BF16)
                    if g[1] == 0 or g[1] == 1:
                        pe.wait_ge(tern_ok, 3)
                        for t, r in enumerate(FROWS):
                            ins = pe.transpose(wb[:, t * P:t * P + r], tern_v[g[1]][0:r, t, g[2] * P:(g[2] + 1) * P],
                                               identb[0:r, 0:r])
                    else:
                        for i in range(3):
                            f = 3 * g[2] + i
                            r = FROWS[f]
                            for m in range(KT):
                                ins = pe.transpose(wb[0:r, i * D + m * P:i * D + (m + 1) * P],
                                                   tern_v[2][:, m, f * P:f * P + r], identb[:, :])
                elif kind == "wo":
                    pe.wait_ge(ctx_ok, g[1] + 1)
                    for i in range(2):
                        t = 2 * g[2] + i
                        for m in range(KT):
                            ins = pe.matmul(w[:, i * D:(i + 1) * D], ctx_c[:, m, t * P:(t + 1) * P], wo_s[:, m, :],
                                            start=m == 0, stop=m == KT - 1)
                elif kind == "x2T":
                    pe.wait_ge(xn2_ok, g[1] + 1)
                    for k in range(KT):
                        for i in range(2):
                            ins = pe.transpose(w[:, k * HALF + i * P:k * HALF + (i + 1) * P],
                                               xn2[:, 2 * g[2] + i, k * P:(k + 1) * P], ident[:, :])
                elif kind == "up":
                    need_empty(pe, ("x2T", g[1], g[2]))
                    m, r = g[3], FROWS[g[3]]
                    for i, wT in enumerate((w1T, w2T)):
                        for k in range(KT):
                            for part in range(2):
                                ins = pe.matmul(w[0:r, i * HALF:(i + 1) * HALF], wT[:, k, m * P:m * P + r],
                                                x2T[:, part, k, :], start=k == 0 and part == 0,
                                                stop=k == KT - 1 and part == 1)
                elif kind == "down":
                    pe.wait_ge(lo_ok, up_no[("up", g[1], g[2], FT - 1)] + 1)
                    for m in range(KT):
                        for f, r in enumerate(FROWS):
                            for part in range(2):
                                ins = pe.matmul(w[:, m * HALF:(m + 1) * HALF], w3T[0:r, f, m * P:(m + 1) * P],
                                                hT[0:r, part, f, :], start=f == 0 and part == 0,
                                                stop=f == FT - 1 and part == 1)
                elif kind == "back":
                    need_empty(pe, ("down", g[1], g[2]))
                    for i in range(2):
                        for m in range(KT):
                            ins = pe.transpose(w[:, i * D + m * P:i * D + (m + 1) * P], yT[:, m, i * P:(i + 1) * P],
                                               ident[:, :])
                ins.then_inc(side_ready, 1)

            def max_turn(u, k):
                i, h, t = max_op(u, k)
                c = units[u][0]
                if k == 0:
                    pe.wait_ge(q_in[u % QSLOTS], 64 * (u // QSLOTS + 1))
                n = piece0[u] + i
                if h == 0 and t == 0:
                    pe.wait_ge(k_in[n % KSLOTS], 80 * (n // KSLOTS + 1))
                need_max_bank(pe, u, k)
                m = (max0[u] + k) % 2
                N = CH if i < c else (t + 1) * P
                pe.matmul(pM[:, m, 0:N], qst[0:R_MAX, u % QSLOTS, h, t * P:(t + 1) * P],
                          kst[0:R_MAX, n % KSLOTS, h, 0:N], start=True, stop=True).then_inc(max_ready, 1)

            def turn_max(u):
                k = max_ops(u)
                need_max_bank(pe, u, k)
                pe.wait_ge(nm_ok, u + 1)
                pe.transpose(pM[0:G * TPC, (max0[u] + k) % 2, 0:P], nm[:, :], ident[:, :]).then_inc(max_ready, 1)

            def scores(s, p):
                u, j = steps[s]
                n = 2 * s + p
                if n >= 2:
                    pe.wait_ge(probs_ready, n - 1)
                if j == 0 and p == 0:
                    pe.wait_ge(m_in, 32 * (u + 1))
                q0 = diag(u, j)
                sl = (piece0[u] + j // TPC) % KSLOTS
                b = j % TPC * P
                for h in (2 * p, 2 * p + 1):
                    ins = pe.matmul(pS[:, h, q0:CH], kst[0:R_END, sl, h, b:b + P], qst[0:R_END, u % QSLOTS, h, q0:CH],
                                    start=True, stop=not is_diag(u, j))
                    if is_diag(u, j):
                        ins = pe.matmul(pS[:, h, q0:q0 + P], identb[:, :], maskb[:, :], start=False, stop=True)
                ins.then_inc(scores_ready, 1)

            def weighted(s):
                u, j = steps[s]
                q0 = diag(u, j)
                if j == 0 and u >= 1:
                    pe.wait_ge(ctx_saved, u)
                pe.wait_ge(probs_ready, 2 * s + 2)
                for h in range(G):
                    n = 2 * s + h // 2
                    ins = pe.matmul(pO[32 * h:32 * h + VW, q0:CH], vals[:, j, units[u][1] * G + h, :],
                                    probs[:, n % PSLOTS, h % 2, q0:CH], start=j == 0, stop=j == n_steps[u] - 1)
                ins.then_inc(pv_done, 1)

            pe.wait_ge(const_ok, 1)
            pe.wait_ge(w_in, 128)
            for g in pre_groups(0):
                side_group(g)
            for k in range(max_ops(0)):
                max_turn(0, k)
            side_group(("gamma",))
            turn_max(0)
            pe.wait_ge(rows_ok, 2)
            for g in head_groups:
                need_empty(pe, g)
            for s, (u, j) in enumerate(steps):
                turns = list(max_share(u, j))
                a, b = len(turns) // 3, 2 * len(turns) // 3
                scores(s, 0)
                for k in turns[:a]:
                    max_turn(u + 1, k)
                scores(s, 1)
                for k in turns[a:b]:
                    max_turn(u + 1, k)
                if j == n_steps[u] - spare(u) and u + 1 < NU:
                    turn_max(u + 1)
                if s:
                    weighted(s - 1)
                for k in turns[b:]:
                    max_turn(u + 1, k)
                if side[s]:
                    side_group(side[s])
            weighted(NS - 1)
            pe.wait_ge(probs_ready, 2 * NS)
            for g in tail_groups:
                side_group(g)

        @block.vector
        def _(dve):
            chain = [0]

            def link(ins):
                chain[0] += 1
                ins.then_inc(vself, 1)
                dve.wait_ge(vself, chain[0])

            def variances(src, t0, t1):
                for t in range(t0, t1):
                    ins = nc.vector.bn_stats(st[:, t, :], src[:, t, :])
                link(ins)
                for t in range(t0, t1):
                    ins = nc.vector.bn_aggr(mv[:, t, :], st[:, t, :])
                link(ins)

            def var_eps():
                nc.vector.tensor_scalar(ve[:, :], mv[:, :, 1], EPS, None, ALU.add).then_inc(var_ok, 1)

            def normalise(dst, src, n):
                dve.wait_ge(rstd_ok, n)
                for t in range(TPC):
                    ins = nc.vector.tensor_scalar(dst[:, t, :], src[:, t, :], mv[:, t, 0:1], rstd[:, t:t + 1],
                                                  ALU.subtract, ALU.mult)
                return ins

            def side_op(g):
                kind = g[0]
                if kind in "kq":
                    i = split_no[g]
                    need_empty(dve, g)
                    if i >= 2:
                        dve.wait_ge(parts_out[i % 2], 32 * (i // 2))
                    hi, lo = qk_hl[:, i % 2, 0, :], qk_hl[:, i % 2, 1, :]
                    link(nc.vector.tensor_copy(hi.bitcast(F32R), qk_f[:, :]))
                    nc.vector.tensor_tensor(lo.bitcast(F32R), qk_f[:, :], hi, ALU.subtract).then_inc(split_ok, 1)
                elif kind == "v":
                    need_side(dve, g)
                    t0 = g[1] * TPC + 2 * g[2]
                    for t in range(2):
                        ins = nc.vector.tensor_tensor(vals[:, t0 + t, :, 0:HD],
                                                      bank(g)[:, t * D:(t + 1) * D].rearrange("p (h d) -> p h d", h=H),
                                                      bv_b[:, :].rearrange("p (h d) -> p h d", h=H), ALU.add)
                    ins.then_inc(side_v, 1)
                elif kind == "w":
                    need_side(dve, g)
                    if g[1] < 2:
                        dst, n = (w1T, w2T)[g[1]][:, g[2], :], FH
                        nc.vector.tensor_scalar(dst, bank(g).bitcast(BF16)[:, 0:n], -1.0, None, ALU.add)\
                            .then_inc(side_v, 1)
                    else:
                        a = 3 * g[2]
                        full = 3 if g[2] == 0 else 2
                        src = bank(g).bitcast(BF16)[:, 0:3 * D].rearrange("p (t n) -> p t n", t=3)
                        ins = nc.vector.tensor_scalar(w3T[:, a:a + full, :], src[:, 0:full, :], -1.0, None, ALU.add)
                        if full == 2:
                            r = FROWS[FT - 1]
                            ins = nc.vector.tensor_scalar(w3T[0:r, FT - 1, :], src[0:r, 2, :], -1.0, None, ALU.add)
                        ins.then_inc(side_v, 1)
                elif kind == "wo":
                    need_side(dve, g)
                    if g[2] == 0:
                        dve.wait_ge(xb_ok, TPC * (g[1] + 1))
                    t0 = 2 * g[2]
                    nc.vector.tensor_tensor(x1[:, t0:t0 + 2, :], bank(g).rearrange("p (t n) -> p t n", t=2),
                                            x1[:, t0:t0 + 2, :], ALU.add).then_inc(side_v, 1)
                    need_empty(dve, g)
                    variances(x1, t0, t0 + 2)
                    if g[2] == 1:
                        var_eps()
                elif kind == "x2T":
                    dve.wait_ge(half_a, half_no[g] + 1)
                    nc.vector.tensor_tensor(x2T[:, 1, :, :], bank(g).rearrange("p (k n) -> p k n", k=KT),
                                            x2T[:, 0, :, :].bitcast(F32), ALU.subtract).then_inc(side_v, 1)
                elif kind == "up":
                    i, m, rows = up_no[g], g[3], FROWS[g[3]]
                    dve.wait_ge(half_a, half_no[g] + 1)
                    if i >= 2:
                        dve.wait_ge(lo_ok, i - 1)
                    nc.vector.scalar_tensor_tensor(out=hid[0:rows, i % 2, :], in0=th[0:rows, i % 2, :], scalar=1.0,
                                                   in1=bank(g)[0:rows, HALF:CH], op0=ALU.add, op1=ALU.mult)\
                        .then_inc(side_v, 1)
                    need_empty(dve, g)
                    if m == 0 and i >= FT:
                        prev = ups[i - 1]
                        need_side(dve, ("down", prev[1], prev[2]))
                    nc.vector.tensor_copy(hT[0:rows, 0, m, :], hid[0:rows, i % 2, :]).then_inc(hid_ok, 1)
                elif kind == "back":
                    need_side(dve, g)
                    n = 2 * g[1] + g[2]
                    if n:
                        dve.wait_ge(out_done, 16 * n)
                    nc.vector.tensor_tensor(fin, bank(g).rearrange("p (t n) -> p t n", t=2),
                                            x1[:, 2 * g[2]:2 * g[2] + 2, :], ALU.add).then_inc(side_v, 1)

            def max_turn(u, k):
                i, h, t = max_op(u, k)
                c = units[u][0]
                m = max0[u] + k
                if k == 0 and u >= 2:
                    dve.wait_ge(nm_ok, u - 1)
                dve.wait_ge(max_ready, m + 1)
                dst = pm[:, u % 2, h * TPC + t, i:i + 1]
                if i < c:
                    nc.vector.tensor_reduce(dst, pM[:, m % 2, :], AX.X, ALU.max).then_inc(max_free, 1)
                else:
                    sc = pM[:, m % 2, 0:(t + 1) * P]
                    nc.vector.tensor_tensor_reduce(out=sc, in0=sc, in1=mask[:, CH - (t + 1) * P:CH], scale=1.0,
                                                   scalar=NEG, op0=ALU.add, op1=ALU.max, accum_out=dst)\
                        .then_inc(max_free, 1)

            def negate(u):
                dve.wait_ge(max_free, turns_before(u) + max_ops(u))
                if u >= 1:
                    dve.wait_ge(max_ready, max0[u])
                nc.vector.tensor_reduce(nm[:, :], pm[:, u % 2, :, 0:units[u][0] + 1], AX.X, ALU.max, negate=True)\
                    .then_inc(nm_ok, 1)

            def split_max(u):
                m = max0[u] + max_ops(u)
                dve.wait_ge(max_ready, m + 1)
                if u >= 1:
                    dve.wait_ge(m_in, 32 * u)
                link(nc.vector.tensor_copy(mT[:, 0, :].bitcast(F32R), pM[0:G * TPC, m % 2, 0:P]))
                nc.vector.tensor_tensor(mT[:, 1, :].bitcast(F32R), pM[0:G * TPC, m % 2, 0:P], mT[:, 0, :],
                                        ALU.subtract).then_inc(mT_ok, 1)

            def norm_ctx(c):
                dve.wait_ge(ctx_in, 16 * 32 * (c + 1))
                link(nc.vector.reciprocal(den_c, den_c))
                nc.vector.tensor_tensor(ctx_c, ctx_c, den_c, ALU.mult).then_inc(ctx_ok, 1)

            dve.wait_ge(al_in, 16)
            link(nc.vector.tensor_copy(al[:, 1, :].bitcast(F32R), al[:, 0, :]))
            link(nc.vector.tensor_tensor(al[:, 2, :].bitcast(F32R), al[:, 0, :], al[:, 1, :], ALU.subtract))
            dve.wait_ge(x_in, 16)
            variances(xin, 0, TPC)
            var_eps()
            nc.vector.memset(kst[64:96, :, :, :].bitcast(F32), 0.0)
            nc.vector.memset(kst[96:98, :, :, :].bitcast(F32), 1.0)
            link(nc.vector.memset(qst[64:96, :, :, :].bitcast(F32), 0.0))
            nc.vector.memset(qst[64:66, :, :, :].bitcast(F32), 1.0).then_inc(rows_ok, 1)
            normalise(xin, xin, 1).then_inc(xn_ok, 1)
            nc.vector.memset(pO[:, :], 0.0)
            nc.vector.memset(vals[:, :, :, HD:VW], 1.0).then_inc(rows_ok, 1)
            dve.wait_ge(w_in, 128)
            for g in head_groups:
                if g[0] in "kq":
                    side_op(g)
            dve.wait_ge(xn_ok, 1)
            dve.wait_ge(x_in, 32)
            variances(xin, 0, TPC)
            var_eps()
            for g in head_groups:
                if g[0] == "v":
                    side_op(g)
            normalise(xin, xin, 2).then_inc(xn_ok, 1)
            for k in range(max_ops(0)):
                max_turn(0, k)
            negate(0)
            split_max(0)
            g = ("gamma",)
            need_side(dve, g)
            link(nc.vector.tensor_scalar(thr[:, 1, 0:3], bank(g)[:, 0:3], 1.0 / (FH * D), QEPS, ALU.mult, ALU.add))
            link(nc.vector.tensor_scalar(thr[:, 0, 0:3], thr[:, 1, 0:3], 0.5, None, ALU.mult))
            nc.vector.tensor_scalar(thr[:, 1, 0:3], thr[:, 0, 0:3], -1.0, None, ALU.mult).then_inc(side_v, 1)
            need_empty(dve, g)
            for i in range(3):
                link(nc.vector.tensor_scalar(tern_v[i], w_rows[i], thr[:, 0, i:i + 1], None, ALU.is_gt))
                nc.vector.scalar_tensor_tensor(out=tern_v[i], in0=w_rows[i], scalar=thr[:, 1, i:i + 1],
                                               in1=tern_v[i], op0=ALU.is_ge, op1=ALU.add).then_inc(tern_ok, 1)
            rstds = 2
            for s, (u, j) in enumerate(steps):
                c = units[u][0]
                ph = s - phase0[c]
                turns = list(max_share(u, j))
                mid = (len(turns) + 1) // 2
                for k in turns[:mid]:
                    max_turn(u + 1, k)
                if j == n_steps[u] - spare(u) and u + 1 < NU:
                    split_max(u + 1)
                if s and side[s - 1]:
                    side_op(side[s - 1])
                if ph == 5 and c >= 1:
                    norm_ctx(c - 1)
                if ph == 12 and c >= 1:
                    rstds += 1
                    normalise(xn2, x1, rstds).then_inc(xn2_ok, 1)
                if ph == LN_AT[c]:
                    dve.wait_ge(x_in, 16 * (c + 3))
                    variances(xin, 0, TPC)
                    var_eps()
                if ph == LN_AT[c] + 2:
                    rstds += 1
                    normalise(xin, xin, rstds).then_inc(xn_ok, 1)
                for k in turns[mid:]:
                    max_turn(u + 1, k)
                if turns and j == n_steps[u] - spare(u) - 1:
                    negate(u + 1)
            if side[NS - 1]:
                side_op(side[NS - 1])
            norm_ctx(NCH - 1)
            for g in tail_groups:
                side_op(g)
                if g[:1] == ("wo",) and g[2] == 1:
                    rstds += 1
                    normalise(xn2, x1, rstds).then_inc(xn2_ok, 1)


_INS = ["L0_attn_x", "L0_attn_Wq", "L0_attn_bq", "L0_attn_Wk", "L0_attn_bk", "L0_attn_Wv", "L0_attn_bv",
        "L0_attn_Wo", "L0_attn_bo", "L0_ffn_w1", "L0_ffn_w2", "L0_ffn_w3"]


def _alibi_table(heads, tokens):
    import numpy as np
    ratio = np.float32(2.0 ** (-8.0 / heads))
    slopes = ratio ** np.arange(1, heads + 1, dtype=np.float32)
    distances = np.arange(1 - tokens, 1, dtype=np.float32)
    return (slopes[:, None] * distances[None, :]).astype(np.float32).reshape(128, -1)


def kernel(**inputs):
    import numpy as _np
    import concourse.bacc as _bacc
    from concourse import mybir as _mybir
    from concourse.bass_utils import run_bass_kernel_spmd as _run

    nc = _bacc.Bacc("TRN2", target_bir_lowering=False, num_devices=1)
    arrays, args = {}, []
    for name in _INS:
        a = _np.ascontiguousarray(inputs[name])
        arrays[f"in_{name}"] = a
        args.append(nc.dram_tensor(f"in_{name}", a.shape, _mybir.dt.from_np(a.dtype), kind="ExternalInput").ap())
    table = _alibi_table(16, inputs["L0_attn_x"].shape[1])
    arrays["alibi"] = table
    args.append(nc.dram_tensor("alibi", table.shape, _mybir.dt.float32, kind="ExternalInput").ap())
    shape = inputs["L0_attn_x"].shape
    args.append(nc.dram_tensor("out_0", shape, _mybir.dt.float32, kind="ExternalOutput").ap())
    preln_layer(nc, *args)
    r = _run(nc, [arrays], core_ids=[0])
    return r.results[0]["out_0"]
```

```python
import concourse.bass as bass
from concourse import mybir
from contextlib import ExitStack



def preln_layer(nc, x, Wq, bq, Wk, bk, Wv, bv, Wo, bo, w1, w2, w3, alibi, out):
    F32, F32R, BF16 = mybir.dt.float32, mybir.dt.float32r, mybir.dt.bfloat16
    ALU = mybir.AluOpType
    ACT = mybir.ActivationFunctionType
    AX = mybir.AxisListType

    _, T, D = x.shape
    FH = w1.shape[0]
    H = 16
    HD = D // H
    P = 128
    CH = 512
    NCH = T // CH
    TPC = CH // P
    G = 4
    NHG = H // G
    KT = D // P
    FT = (FH + P - 1) // P
    FROWS = [min(P, FH - i * P) for i in range(FT)]
    HALF = CH // 2
    EPS = 1e-5
    QEPS = 1e-8
    NEG = -3.0e38
    VW = HD + 1
    R_ALIBI = 4 * HD
    R_MAX = 96
    R_END = R_MAX + 2
    KSLOTS, QSLOTS, PSLOTS = 8, 3, 7
    SBANKS, MBANKS = 3, 3
    K_DMAS, Q_DMAS, PART_DMAS = 2, 3, 2 * (P // (G * HD))

    units = [(c, hg) for c in range(NCH) for hg in range(NHG)]
    NU = len(units)
    n_steps = [TPC * (c + 1) for c, _ in units]
    first_step = [sum(n_steps[:u]) for u in range(NU + 1)]
    NS = first_step[NU]
    phase0 = [first_step[c * NHG] for c in range(NCH)] + [NS]
    steps = [(u, j) for u in range(NU) for j in range(n_steps[u])]

    piece0 = [sum(units[v][0] + 1 for v in range(u)) for u in range(NU + 1)]
    pieces = [(u, i) for u in range(NU) for i in range(units[u][0] + 1)]

    def n_turns(u):
        return G * TPC * (units[u][0] + 1)

    def turn_of(u, k):
        return k // (G * TPC), k // TPC % G, k % TPC

    def swap_step(u):
        v = u - 1
        return first_step[u] - (3 if n_steps[v] > TPC else 2)

    def turns_start(u):
        s0 = swap_step(u - 1) if u >= 2 else 0
        c, hg = units[u]
        return max(s0, phase0[c - 1] + 10) if hg == 0 and c >= 1 else s0

    step_turns = [[] for _ in range(NS)]
    step_swap = [None] * NS
    for u in range(1, NU):
        a, b = turns_start(u), swap_step(u)
        for s in range(a, b):
            step_turns[s] += [(u, k) for k in range(n_turns(u) * (s - a) // (b - a),
                                                     n_turns(u) * (s - a + 1) // (b - a))]
        step_swap[b] = u
    def turns_after(s, h):
        t = step_turns[s]
        return t[(len(t) * h + G - 1) // G:(len(t) * (h + 1) + G - 1) // G]

    bank_use = [("turn", 0, k) for k in range(n_turns(0))] + [("swap", 0)]
    for s in range(NS):
        bank_use += [("turn", *use) for use in step_turns[s]]
        bank_use += [("swap", step_swap[s])] if step_swap[s] else []
    use_no = {x: i for i, x in enumerate(bank_use)}
    turns_to = [0]
    for use in bank_use:
        turns_to.append(turns_to[-1] + (use[0] == "turn"))

    def pre_groups(c):
        return ([("xT", c, k) for k in range(KT)] + [("k", c, m) for m in range(KT)]
                + [("q", c, m) for m in range(KT)] + [("v", c, i) for i in range(TPC // 2)])

    weight_groups = [("w", i, k) for i in range(3) for k in range(2)]

    def post_groups(c):
        up = [[("up", c, h, m) for m in range(FT)] for h in range(2)]
        return ([("wo", c, 0), ("wo", c, 1), None, None, ("x2T", c, 0)] + up[0]
                + [("x2T", c, 1), ("down", c, 0), up[1][0], ("back", c, 0)] + up[1][1:]
                + [None, ("down", c, 1), None, ("back", c, 1)])

    POST_AT = [None, 8, 8, 56]
    side = [None] * NS
    spill = []
    for c in range(NCH):
        lst = pre_groups(c + 1) if c + 1 < NCH else []
        lst = lst + (weight_groups if c == 0 else [None] * (POST_AT[c] - len(lst)) + post_groups(c - 1))
        for i, g in enumerate(lst):
            if phase0[c] + i < NS:
                side[phase0[c] + i] = g
            elif g:
                spill.append(g)
    head_groups = pre_groups(0)
    head_groups[-2:-2] = [("gamma",)]
    tail_groups = spill + [g for g in post_groups(NCH - 1) if g]
    order = head_groups + [g for g in side if g] + tail_groups
    number = {g: i for i, g in enumerate(order)}
    READS_LAST = {"gamma": "v", "xT": "a", "k": "a", "q": "a", "v": "v", "w": "v", "wo": "v",
                  "x2T": "v", "up": "v", "down": "a", "back": "v"}
    NHEAD, NTAIL0 = len(head_groups), len(order) - len(tail_groups)
    bank_of, prev_user, emptied = [], [], []
    last = {}
    for i, g in enumerate(order):
        b = i % (1 + SBANKS) if i < NHEAD else (i - NTAIL0) % (1 + SBANKS) if i >= NTAIL0 else 0
        bank_of.append(b)
        prev_user.append(last.get(b))
        last[b] = i
        e = READS_LAST[g[0]]
        emptied.append((e, 1 + sum(READS_LAST[q[0]] == e for q in order[:i])))
    LN_AT = {0: 10, 1: 20, 2: -9, 3: -9}
    splits = [g for g in order if g[0] in "kq"]
    split_no = {g: i for i, g in enumerate(splits)}
    halves = [g for g in order if g[0] in ("x2T", "up")]
    half_no = {g: i for i, g in enumerate(halves)}
    ups = [g for g in order if g[0] == "up"]
    up_no = {g: i for i, g in enumerate(ups)}

    parts = nc.dram_tensor("parts", (2, NCH, NHG, 2, HD, G, CH), F32, kind="Internal").ap()
    alibi_parts = nc.dram_tensor("alibi_parts", (2, H, T), F32, kind="Internal").ap()
    rden_dram = nc.dram_tensor("rden_dram", (NCH, H, CH), F32, kind="Internal").ap()
    ctx_dram = nc.dram_tensor("ctx_dram", (NCH, NHG, G, 32, CH), F32, kind="Internal").ap()

    es = ExitStack()
    with es:
        def sb(name, shape, dt=F32):
            return es.enter_context(nc.sbuf_tensor(name, shape, dt))

        def sem(name):
            return es.enter_context(nc.semaphore(name))

        kst = sb("kst", [P, KSLOTS, G, CH], F32R)
        qst = sb("qst", [P, QSLOTS, G, CH], F32R)
        probs = sb("probs", [P, PSLOTS, CH])
        vals = sb("vals", [P, T // P, H, VW])
        xin = sb("xin", [P, TPC, D])
        xnT = sb("xnT", [P, KT, CH])
        wq_s, wk_s, wv_s, wo_s = (sb(n, [P, KT, D]) for n in ("wq_s", "wk_s", "wv_s", "wo_s"))
        w1T, w2T = sb("w1T", [P, KT, FH], F32R), sb("w2T", [P, KT, FH], F32R)
        w3T = sb("w3T", [P, FT, D], F32R)
        qk_f = sb("qk_f", [P, CH])
        qk_hl = sb("qk_hl", [P, 2, 2, CH])
        ctx_raw = sb("ctx_raw", [P, CH])
        work = sb("work", [P, 5120])
        ctx_c = work[:, 0:1024].rearrange("p (m n) -> p m n", m=KT)
        den_c = work[:, 1024:2048].rearrange("p (m n) -> p m n", m=KT)
        xn2 = work[:, 1024:2048].rearrange("p (t n) -> p t n", t=TPC)
        x1 = work[:, 2048:3072].rearrange("p (t n) -> p t n", t=TPC)
        th = work[:, 3072:3584].rearrange("p (i n) -> p i n", i=2)
        hid = work[:, 3584:4096].rearrange("p (i n) -> p i n", i=2)
        yT = work[:, 4096:4608].rearrange("p (m n) -> p m n", m=KT)
        fin = work[:, 4608:5120].rearrange("p (t n) -> p t n", t=2)
        w_rows = [probs[:, :, :].rearrange("p a n -> p (a n)")[:, 0:FT * D].rearrange("p (t n) -> p t n", n=D),
                  probs[:, :, :].rearrange("p a n -> p (a n)")[:, FT * D:2 * FT * D].rearrange("p (t n) -> p t n", n=D),
                  work[:, 0:KT * FH].rearrange("p (t n) -> p t n", n=FH)]
        al = work[:, 5120 - 3 * H * T // P:5120].rearrange("p (a n) -> p a n", a=3)
        ones = work[:, 4096:4096 + P]
        tern0 = KT * FH
        tern = [work[:, tern0 + i * FT * D // 2:tern0 + (i + 1) * FT * D // 2].bitcast(BF16) for i in range(2)]
        tern.append(work[:, tern0 + FT * D:tern0 + FT * D + KT * FH // 2].bitcast(BF16))
        tern_v = [tern[0].rearrange("p (t n) -> p t n", n=D), tern[1].rearrange("p (t n) -> p t n", n=D),
                  tern[2].rearrange("p (t n) -> p t n", n=FH)]
        x2T = sb("x2T", [P, 2, KT, HALF], F32R)
        hT = sb("hT", [P, 2, FT, HALF], F32R)
        mask = sb("mask", [P, CH], BF16)
        maskb = sb("maskb", [P, P], BF16)
        ident = sb("ident", [P, P])
        identb = sb("identb", [P, P], BF16)
        bias_q, bias_k = sb("bias_q", [P, KT]), sb("bias_k", [P, KT])
        bv_b, bo_b = sb("bv_b", [P, D]), sb("bo_b", [P, D])
        bq_raw = sb("bq_raw", [P, KT])
        wsum = sb("wsum", [P, 4])
        thr = sb("thr", [P, 2, 4])
        st = sb("st", [P, TPC, 6])
        mv = sb("mv", [P, TPC, 2])
        ve = sb("ve", [P, TPC])
        mhalf = sb("mhalf", [P, TPC])
        rstd = sb("rstd", [P, TPC])
        pm = sb("pm", [P, 2, G * TPC, NCH])
        nm = sb("nm", [P, G * TPC])
        dens = sb("dens", [P, H * CH // P])
        mT = sb("mT", [G * TPC, 2, P])

        pS = es.enter_context(nc.psum_tensor("pS", [P, SBANKS, CH], F32))
        pO = es.enter_context(nc.psum_tensor("pO", [P, CH], F32))
        pM = es.enter_context(nc.psum_tensor("pM", [P, MBANKS, CH], F32))
        pW = es.enter_context(nc.psum_tensor("pW", [P, CH], F32))

        def x1_of(c):
            return x1 if c < NCH - 1 else xin[:, :, :]

        def bank(g):
            b = bank_of[number[g]]
            return pW[:, :] if b == 0 else pS[:, b - 1, :]

        x_in = sem("x_in")
        w_in = sem("w_in")
        raw_in = sem("raw_in")
        al_in = sem("al_in")
        al_out = sem("al_out")
        x1_in = sem("x1_in")
        xlast_in = sem("xlast_in")
        const_ok = sem("const_ok")
        pad_ok = sem("pad_ok")
        rows_ok = sem("rows_ok")
        k_rows = sem("k_rows")
        q_rows = sem("q_rows")
        vself = sem("vself")
        pself = sem("pself")
        var_ok = sem("var_ok")
        rstd_ok = sem("rstd_ok")
        xn_ok = sem("xn_ok")
        xn2_ok = sem("xn2_ok")
        wsum_ok = sem("wsum_ok")
        tern_ok = sem("tern_ok")
        side_ready = sem("side_ready")
        side_a = sem("side_a")
        side_v = sem("side_v")
        half_a = sem("half_a")
        split_ok = sem("split_ok")
        parts_out = [sem(f"parts_out{i}") for i in range(2)]
        k_in = [sem(f"k_in{i}") for i in range(KSLOTS)]
        q_in = [sem(f"q_in{i}") for i in range(QSLOTS)]
        m_in = sem("m_in")
        max_ready = sem("max_ready")
        max_free = sem("max_free")
        nm_ok = sem("nm_ok")
        mT_ok = sem("mT_ok")
        scores_ready = sem("scores_ready")
        probs_ready = sem("probs_ready")
        pv_done = sem("pv_done")
        ctx_saved = sem("ctx_saved")
        ctx_out = sem("ctx_out")
        ctx_in = sem("ctx_in")
        den_in = sem("den_in")
        rden_ok = sem("rden_ok")
        rden_out = sem("rden_out")
        ctx_ok = sem("ctx_ok")
        xb_ok = sem("xb_ok")
        hid_ok = sem("hid_ok")
        lo_ok = sem("lo_ok")
        out_done = sem("out_done")

        block = es.enter_context(nc.Block())

        def diag(u, j):
            return max(0, j - TPC * units[u][0]) * P

        def is_diag(u, j):
            return j >= TPC * units[u][0]

        def max_bank(x):
            return pM[:, use_no[x] % MBANKS, :]

        def need_max_bank(eng, x):
            i = use_no[x] - MBANKS
            if i >= 0 and bank_use[i][0] == "turn":
                eng.wait_ge(max_free, turns_to[i + 1])
            elif i >= 0:
                eng.wait_ge(mT_ok, bank_use[i][1] + 1)

        def need_side(eng, g):
            eng.wait_ge(side_ready, number[g] + 1)

        def need_empty(eng, g):
            e, n = emptied[number[g]]
            eng.wait_ge(side_a if e == "a" else side_v, n)

        @block.sync
        def _(sp):
            def load_x(c):
                if c >= 1:
                    need_side(sp, ("xT", c - 1, KT - 1))
                sp.dma_start(xin[:, :, :], x[0, c * CH:(c + 1) * CH, :].rearrange("(t p) d -> p t d", p=P))\
                    .then_inc(x_in, 16)

            def load_x1(c):
                if c == 0:
                    need_side(sp, weight_groups[-1])
                elif c < NCH - 1:
                    need_empty(sp, ("back", c - 1, 1))
                else:
                    need_side(sp, ("xT", c, KT - 1))
                sp.dma_start(x1_of(c), x[0, c * CH:(c + 1) * CH, :].rearrange("(t p) d -> p t d", p=P))\
                    .then_inc(x1_in if c < NCH - 1 else xlast_in, 16)

            def store_parts(g):
                i = split_no[g]
                w = 0 if g[0] == "q" else 1
                sp.wait_ge(split_ok, i + 1)
                for part in range(2):
                    for a in range(P // (G * HD)):
                        sp.dma_start(parts[w, g[1], g[2] * (P // (G * HD)) + a, part, :, :, :]
                                     .rearrange("d h n -> h d n"),
                                     qk_hl[a * G * HD:(a + 1) * G * HD, i % 2, part, :])\
                            .then_inc(parts_out[i % 2], 16)

            def parts_there(c):
                for i in range(2):
                    n = sum(split_no[g] % 2 == i for g in splits if g[1] <= c)
                    sp.wait_ge(parts_out[i], PART_DMAS * 16 * n)

            def load_k(n):
                v, i = pieces[n]
                parts_there(i)
                if n >= KSLOTS:
                    pu, pi = pieces[n - KSLOTS]
                    sp.wait_ge(scores_ready, G * (first_step[pu] + TPC * pi + TPC))
                if n < KSLOTS:
                    sp.wait_ge(k_rows, n + 1)
                hg = units[v][1]
                src = parts[1, i, hg, :, :, :, :].rearrange("(a p) d h n -> a (p d) (h n)", a=1)
                sp.dma_start(kst[0:4 * HD, n % KSLOTS, :, :].bitcast(F32).rearrange("r h n -> r (h n)"),
                             src.to_broadcast([2, 2 * HD, G * CH])).then_inc(k_in[n % KSLOTS], 16)
                sp.dma_start(kst[R_ALIBI:R_ALIBI + 2, n % KSLOTS, :, :].bitcast(F32),
                             alibi_parts[:, hg * G:(hg + 1) * G, i * CH:(i + 1) * CH])\
                    .then_inc(k_in[n % KSLOTS], 16)

            def load_q(v):
                c, hg = units[v]
                parts_there(c)
                if v >= QSLOTS:
                    sp.wait_ge(scores_ready, G * first_step[v - QSLOTS + 1])
                if v < QSLOTS:
                    sp.wait_ge(q_rows, v + 1)
                src = parts[0, c, hg, :, :, :, :]
                dst = qst[:, v % QSLOTS, :, :].bitcast(F32).rearrange("r h n -> r (h n)")
                sp.dma_start(dst[0:2 * HD, :], src.rearrange("p d h n -> (p d) (h n)"))\
                    .then_inc(q_in[v % QSLOTS], 16)
                for b in range(2):
                    sp.dma_start(dst[(2 + b) * HD:(3 + b) * HD, :],
                                 src[1 - b, :, :, :].rearrange("d h n -> d (h n)"))\
                        .then_inc(q_in[v % QSLOTS], 16)

            def load_m(v):
                sp.wait_ge(mT_ok, v + 1)
                for part in range(2):
                    sp.dma_start(qst[R_MAX + part:R_MAX + part + 1, v % QSLOTS, :, :].bitcast(F32)
                                 .rearrange("o h (t n) -> o (h t) n", n=P),
                                 mT[:, part, :]).then_inc(m_in, 16)

            def store_ctx(u):
                sp.wait_ge(ctx_saved, u + 1)
                c, hg = units[u]
                sp.dma_start(ctx_dram[c, hg, :, :, :].rearrange("h r n -> (h r) n"), ctx_raw[:, :])\
                    .then_inc(ctx_out, 16)

            def load_ctx(c):
                sp.wait_ge(ctx_out, 16 * NHG * (c + 1))
                need_side(sp, ("wo", c - 1, 1) if c >= 1 else weight_groups[-1])
                by_head = ctx_dram[c, :, :, :, :].rearrange("g h r n -> (g h) r n")
                sp.dma_start(dens[:, :], by_head[:, HD, :].rearrange("h (i n) -> h i n", i=P // H))\
                    .then_inc(den_in, 16)
                for m in range(KT):
                    sp.dma_start(ctx_c[:, m, :], by_head[m * P // HD:(m + 1) * P // HD, 0:HD, :])\
                        .then_inc(ctx_in, 16)

            def spread_rden(c):
                sp.wait_ge(rden_ok, c + 1)
                sp.dma_start(rden_dram[c, :, :].rearrange("h (i n) -> (h i) n", i=P // H), dens[:, :])\
                    .then_inc(rden_out, 16)
                sp.wait_ge(rden_out, 16 * (c + 1))
                if c >= 1:
                    need_side(sp, ("x2T", c - 1, 1))
                for m in range(KT):
                    rows = rden_dram[c, m * P // HD:(m + 1) * P // HD, :].rearrange("h (a n) -> h a n", a=1)
                    sp.dma_start(den_c[:, m, :], rows.to_broadcast([P // HD, HD, CH])).then_inc(ctx_in, 16)

            def store_out(c, h):
                need_empty(sp, ("back", c, h))
                t0 = c * CH + h * HALF
                sp.dma_start(out[0, t0:t0 + HALF, :].rearrange("(t p) d -> p t d", p=P), fin)\
                    .then_inc(out_done, 16)

            load_x(0)
            sp.dma_start(al[:, 0, :], alibi).then_inc(al_in, 16)
            for dst, src in ((wk_s, Wk), (wq_s, Wq), (wv_s, Wv), (wo_s, Wo)):
                sp.dma_start(dst[:, :, :], src.rearrange("(k p) n -> p k n", p=P)).then_inc(w_in, 16)
            for dst, src in ((bq_raw, bq), (bias_k, bk)):
                sp.dma_start(dst[:, :], src.rearrange("(m p) -> p m", p=P), allow_slow_non_contiguous=True)\
                    .then_inc(w_in, 16)
            for dst, src in ((bv_b, bv), (bo_b, bo)):
                sp.dma_start(dst[:, :], src.rearrange("(a n) -> a n", a=1).to_broadcast([P, D]))\
                    .then_inc(w_in, 16)
            sp.wait_ge(pad_ok, 1)
            FF = (FT - 1) * P
            for i, w in enumerate((w1, w2)):
                sp.dma_start(w_rows[i][:, 0:FT - 1, :], w[0:FF, :].rearrange("(t p) n -> p t n", p=P))\
                    .then_inc(raw_in, 16)
                sp.dma_start(w_rows[i][0:FH - FF, FT - 1, :], w[FF:FH, :]).then_inc(raw_in, 16)
            sp.dma_start(w_rows[2], w3.rearrange("(t p) n -> p t n", p=P)).then_inc(raw_in, 16)
            sp.wait_ge(vself, 2)
            for part in range(2):
                sp.dma_start(alibi_parts[part, :, :].rearrange("h (i n) -> (h i) n", n=H * T // P),
                             al[:, 1 + part, :]).then_inc(al_out, 16)
            load_x(1)
            for g in pre_groups(0):
                if g[0] in "kq":
                    store_parts(g)
            sp.wait_ge(al_out, 32)
            for n in range(2):
                load_k(n)
                load_q(n)
            load_m(0)

            k_at, q_at = {}, {}
            for n in range(2, len(pieces)):
                v, i = pieces[n]
                c = units[v][0]
                s = 0
                if n >= KSLOTS:
                    pu, pi = pieces[n - KSLOTS]
                    s = first_step[pu] + TPC * pi + TPC - 1
                if c >= 1:
                    s = max(s, phase0[c - 1] + 8)
                k_at.setdefault(s, []).append(n)
            for v in range(2, NU):
                c = units[v][0]
                s = first_step[v - QSLOTS + 1] - 1 if v >= QSLOTS else 0
                if c >= 1:
                    s = max(s, phase0[c - 1] + 8)
                q_at.setdefault(s, []).append(v)
            for s, (u, j) in enumerate(steps):
                c, hg = units[u]
                ph = s - phase0[c]
                g = side[s - 1] if s else None
                if g and g[0] in "kq":
                    store_parts(g)
                if g and g[0] == "back":
                    store_out(g[1], g[2])
                for n in k_at.get(s, []):
                    load_k(n)
                for v in q_at.get(s, []):
                    load_q(v)
                if step_swap[s]:
                    load_m(step_swap[s])
                if j == 0 and u >= 1:
                    store_ctx(u - 1)
                if ph == 1 and c >= 1:
                    load_ctx(c - 1)
                    load_x1(c - 1)
                    if c == NCH - 1:
                        load_x1(c)
                if ph == 3 and c + 2 < NCH:
                    load_x(c + 2)
                if ph == 4 and c >= 1:
                    spread_rden(c - 1)
            store_ctx(NU - 1)
            load_ctx(NCH - 1)
            spread_rden(NCH - 1)
            for g in tail_groups:
                if g[0] == "back":
                    store_out(g[1], g[2])
            sp.wait_ge(out_done, 16 * 2 * NCH)

        @block.gpsimd
        def _(pool):
            chain = [0]

            def link(ins):
                chain[0] += 1
                ins.then_inc(pself, 1)
                pool.wait_ge(pself, chain[0])

            link(nc.gpsimd.memset(mhalf[:, :], -0.5))
            for i in range(2):
                ins = nc.gpsimd.memset(w_rows[i][FROWS[FT - 1]:P, FT - 1, :], 0.0)
            ins.then_inc(pad_ok, 1)
            pool.wait_ge(pad_ok, 1)
            link(nc.gpsimd.memset(ident[:, :], 0.0))
            link(nc.gpsimd.affine_select(out=ident[:, :], in_=ident[:, :], compare_op=ALU.not_equal, fill=1.0,
                                         base=0, pattern=[[-1, P]], channel_multiplier=1))
            link(nc.gpsimd.tensor_copy(identb[:, :], ident[:, :]))
            link(nc.gpsimd.memset(mask[:, :], 0.0))
            link(nc.gpsimd.affine_select(out=mask[:, CH - P:CH], in_=mask[:, CH - P:CH], compare_op=ALU.is_ge,
                                         fill=NEG, base=0, pattern=[[-1, P]], channel_multiplier=1))
            link(nc.gpsimd.memset(maskb[:, :], 0.0))
            link(nc.gpsimd.affine_select(out=maskb[:, :], in_=maskb[:, :], compare_op=ALU.is_ge, fill=NEG,
                                         base=0, pattern=[[1, P]], channel_multiplier=-1))
            nc.gpsimd.memset(ones, 1.0).then_inc(const_ok, 1)

            pool.wait_ge(const_ok, 1)

            def power(n):
                pool.wait_ge(var_ok, n)
                nc.gpsimd.tensor_tensor(rstd[:, :], ve[:, :], mhalf[:, :], ALU.pow).then_inc(rstd_ok, 1)
                pool.wait_ge(rstd_ok, n)

            def add_bo(c):
                if c < NCH - 1:
                    pool.wait_ge(x1_in, 16 * (c + 1))
                else:
                    pool.wait_ge(xlast_in, 16)
                for t in range(TPC):
                    ins = nc.gpsimd.tensor_tensor(x1_of(c)[:, t, :], x1_of(c)[:, t, :], bo_b[:, :], ALU.add)
                    ins.then_inc(xb_ok, 1)
                    pool.wait_ge(xb_ok, TPC * c + t + 1)

            def lo_part(g):
                i, m, rows = up_no[g], g[3], FROWS[g[3]]
                pool.wait_ge(hid_ok, i + 1)
                nc.gpsimd.tensor_tensor(hT[0:rows, 1, m, :], hid[0:rows, i % 2, :],
                                        hT[0:rows, 0, m, :].bitcast(F32), ALU.subtract).then_inc(lo_ok, 1)
                pool.wait_ge(lo_ok, i + 1)

            def key_rows(n):
                nc.gpsimd.memset(kst[R_ALIBI:R_END, n, :, :].bitcast(F32), 1.0).then_inc(k_rows, 1)
                pool.wait_ge(k_rows, n + 1)

            def query_rows(n):
                link(nc.gpsimd.memset(qst[R_ALIBI:R_MAX, n, :, :].bitcast(F32), 0.0))
                nc.gpsimd.memset(qst[R_ALIBI:R_ALIBI + 2, n, :, :].bitcast(F32), 1.0).then_inc(q_rows, 1)
                pool.wait_ge(q_rows, n + 1)

            def split_lo(g):
                i = split_no[g]
                need_empty(pool, g)
                hi, lo = qk_hl[:, i % 2, 0, :], qk_hl[:, i % 2, 1, :]
                nc.gpsimd.tensor_tensor(lo.bitcast(F32R), qk_f[:, :], hi, ALU.subtract).then_inc(split_ok, 1)
                pool.wait_ge(split_ok, i + 1)

            key_rows(0)
            power(1)
            query_rows(0)
            key_rows(1)
            query_rows(1)
            for g in head_groups:
                if g[0] in "kq":
                    split_lo(g)
            power(2)
            query_rows(2)
            for n in range(2, KSLOTS):
                key_rows(n)
            powers = 2
            pool.wait_ge(w_in, 128)
            for s, (u, j) in enumerate(steps):
                c = units[u][0]
                ph = s - phase0[c]
                g = side[s]
                if g and g[0] in "kq":
                    split_lo(g)
                if g and g[0] == "up":
                    lo_part(g)
                if ph == 2 and c >= 1:
                    add_bo(c - 1)
                if ph == 2 and c == NCH - 1:
                    add_bo(c)
                if (c >= 1 and ph == POST_AT[c] + 2) or ph == LN_AT[c] + 1:
                    powers += 1
                    power(powers)
            for g in tail_groups:
                if g[0] == "up":
                    lo_part(g)
                if g == ("wo", NCH - 1, 1):
                    power(powers + 1)

        @block.scalar
        def _(act):
            def side_op(g):
                kind = g[0]
                if kind == "xT":
                    need_side(act, g)
                    if g[1] >= 1:
                        need_side(act, ("v", g[1] - 1, 1))
                    nc.scalar.activation(xnT[:, g[2], :], bank(g), ACT.Copy).then_inc(side_a, 1)
                elif kind in "kq":
                    need_side(act, g)
                    i = split_no[g]
                    if i >= 1:
                        act.wait_ge(split_ok, i)
                    if i >= 2:
                        act.wait_ge(parts_out[i % 2], PART_DMAS * 16 * (i // 2))
                    b, sc = (bias_k, 1.0) if kind == "k" else (bias_q, HD ** -0.5)
                    nc.scalar.activation(qk_f[:, :], bank(g), ACT.Identity, bias=b[:, g[2]:g[2] + 1], scale=sc)
                    nc.scalar.activation(qk_hl[:, i % 2, 0, :].bitcast(F32R), bank(g), ACT.Identity,
                                         bias=b[:, g[2]:g[2] + 1], scale=sc).then_inc(side_a, 1)
                elif kind == "x2T":
                    need_side(act, g)
                    if g[2] == 1 or g[1] >= 1:
                        need_side(act, ("up", g[1] - 1 + g[2], 1 - g[2], FT - 1))
                    nc.scalar.activation(x2T[:, 0, :, :], bank(g).rearrange("p (k n) -> p k n", k=KT), ACT.Copy)\
                        .then_inc(half_a, 1)
                elif kind == "up":
                    i, rows = up_no[g], FROWS[g[3]]
                    need_side(act, g)
                    if i >= 2:
                        act.wait_ge(hid_ok, i - 1)
                    nc.scalar.activation(th[0:rows, i % 2, :], bank(g)[0:rows, 0:HALF], ACT.Tanh, scale=0.5)\
                        .then_inc(half_a, 1)
                elif kind == "down":
                    need_side(act, g)
                    if g[2] == 1 or g[1] >= 1:
                        need_side(act, ("back", g[1] - 1 + g[2], 1 - g[2]))
                    nc.scalar.activation(yT, bank(g).rearrange("p (m n) -> p m n", m=KT), ACT.Copy, scale=0.5)\
                        .then_inc(side_a, 1)

            def exps(s, h):
                u, j = steps[s]
                n = G * s + h
                q0 = diag(u, j)
                act.wait_ge(scores_ready, n + 1)
                if n >= PSLOTS:
                    act.wait_ge(pv_done, n - PSLOTS + 1)
                if n == 0:
                    act.wait_ge(tern_ok, 3)
                nc.scalar.activation(probs[:, n % PSLOTS, q0:CH], pS[:, n % SBANKS, q0:CH], ACT.Exp)\
                    .then_inc(probs_ready, 1)

            def save_ctx(u):
                act.wait_ge(pv_done, G * first_step[u + 1])
                if u >= 1:
                    act.wait_ge(ctx_out, 16 * u)
                nc.scalar.activation(ctx_raw[:, :], pO[:, :], ACT.Copy).then_inc(ctx_saved, 1)

            act.wait_ge(w_in, 128)
            nc.scalar.mul(bias_q[:, :], bq_raw[:, :], HD ** -0.5).then_inc(wsum_ok, 1)
            act.wait_ge(wsum_ok, 1)
            for g in head_groups:
                if g[0] in ("xT", "k", "q"):
                    side_op(g)
            act.wait_ge(raw_in, 80)
            for i in range(3):
                wr = w_rows[i].rearrange("p t n -> p (t n)")
                nc.scalar.activation(tern[i], wr, ACT.Abs, accum_out=wsum[:, i:i + 1])\
                    .then_inc(wsum_ok, 1)
            for s, (u, j) in enumerate(steps):
                for h in range(G):
                    exps(s, h)
                    if h == 2 and side[s]:
                        side_op(side[s])
                if j == 0 and u >= 1:
                    save_ctx(u - 1)
            save_ctx(NU - 1)
            for g in tail_groups:
                side_op(g)

        @block.tensor
        def _(pe):
            def side_group(g):
                kind = g[0]
                if prev_user[number[g]] is not None:
                    need_empty(pe, order[prev_user[number[g]]])
                w = bank(g)
                if kind == "xT":
                    pe.wait_ge(xn_ok, g[1] + 1)
                    for t in range(TPC):
                        ins = pe.transpose(w[:, t * P:(t + 1) * P], xin[:, t, g[2] * P:(g[2] + 1) * P], ident[:, :])
                elif kind in "kq":
                    need_empty(pe, ("xT", g[1], KT - 1))
                    for k in range(KT):
                        ins = pe.matmul(w, (wk_s if kind == "k" else wq_s)[:, k, g[2] * P:(g[2] + 1) * P],
                                        xnT[:, k, :], start=k == 0, stop=k == KT - 1)
                elif kind == "v":
                    for i in range(2):
                        t = 2 * g[2] + i
                        for k in range(KT):
                            ins = pe.matmul(w[:, i * D:(i + 1) * D], xnT[:, k, t * P:(t + 1) * P], wv_s[:, k, :],
                                            start=k == 0, stop=k == KT - 1)
                elif kind == "gamma":
                    pe.wait_ge(wsum_ok, 4)
                    ins = pe.matmul(w[:, 0:3], ones, wsum[:, 0:3], start=True, stop=True)
                elif kind == "w":
                    wb = w.bitcast(BF16)
                    if g[1] == 0 or g[1] == 1:
                        pe.wait_ge(tern_ok, 3)
                        for t, r in enumerate(FROWS):
                            ins = pe.transpose(wb[:, t * P:t * P + r], tern_v[g[1]][0:r, t, g[2] * P:(g[2] + 1) * P],
                                               identb[0:r, 0:r])
                    else:
                        for i in range(3):
                            f = 3 * g[2] + i
                            r = FROWS[f]
                            for m in range(KT):
                                ins = pe.transpose(wb[0:r, i * D + m * P:i * D + (m + 1) * P],
                                                   tern_v[2][:, m, f * P:f * P + r], identb[:, :])
                elif kind == "wo":
                    pe.wait_ge(ctx_ok, g[1] + 1)
                    for i in range(2):
                        t = 2 * g[2] + i
                        for m in range(KT):
                            ins = pe.matmul(w[:, i * D:(i + 1) * D], ctx_c[:, m, t * P:(t + 1) * P], wo_s[:, m, :],
                                            start=m == 0, stop=m == KT - 1)
                elif kind == "x2T":
                    pe.wait_ge(xn2_ok, g[1] + 1)
                    for k in range(KT):
                        for i in range(2):
                            ins = pe.transpose(w[:, k * HALF + i * P:k * HALF + (i + 1) * P],
                                               xn2[:, 2 * g[2] + i, k * P:(k + 1) * P], ident[:, :])
                elif kind == "up":
                    need_empty(pe, ("x2T", g[1], g[2]))
                    m, r = g[3], FROWS[g[3]]
                    for i, wT in enumerate((w1T, w2T)):
                        for k in range(KT):
                            for part in range(2):
                                ins = pe.matmul(w[0:r, i * HALF:(i + 1) * HALF], wT[:, k, m * P:m * P + r],
                                                x2T[:, part, k, :], start=k == 0 and part == 0,
                                                stop=k == KT - 1 and part == 1)
                elif kind == "down":
                    pe.wait_ge(lo_ok, up_no[("up", g[1], g[2], FT - 1)] + 1)
                    for m in range(KT):
                        for f, r in enumerate(FROWS):
                            for part in range(2):
                                ins = pe.matmul(w[:, m * HALF:(m + 1) * HALF], w3T[0:r, f, m * P:(m + 1) * P],
                                                hT[0:r, part, f, :], start=f == 0 and part == 0,
                                                stop=f == FT - 1 and part == 1)
                elif kind == "back":
                    need_empty(pe, ("down", g[1], g[2]))
                    for i in range(2):
                        for m in range(KT):
                            ins = pe.transpose(w[:, i * D + m * P:i * D + (m + 1) * P], yT[:, m, i * P:(i + 1) * P],
                                               ident[:, :])
                ins.then_inc(side_ready, 1)

            def max_turn(u, k):
                i, h, t = turn_of(u, k)
                c = units[u][0]
                if k == 0:
                    pe.wait_ge(q_in[u % QSLOTS], Q_DMAS * 16 * (u // QSLOTS + 1))
                n = piece0[u] + i
                if h == 0 and t == 0:
                    pe.wait_ge(k_in[n % KSLOTS], K_DMAS * 16 * (n // KSLOTS + 1))
                x = ("turn", u, k)
                need_max_bank(pe, x)
                N = CH if i < c else (t + 1) * P
                pe.matmul(max_bank(x)[:, 0:N], qst[0:R_MAX, u % QSLOTS, h, t * P:(t + 1) * P],
                          kst[0:R_MAX, n % KSLOTS, h, 0:N], start=True, stop=True).then_inc(max_ready, 1)

            def swap_max(u):
                x = ("swap", u)
                need_max_bank(pe, x)
                pe.wait_ge(nm_ok, u + 1)
                pe.transpose(max_bank(x)[0:G * TPC, 0:P], nm[:, :], ident[:, :]).then_inc(max_ready, 1)

            def scores(s, h):
                u, j = steps[s]
                n = G * s + h
                if n >= SBANKS:
                    pe.wait_ge(probs_ready, n - SBANKS + 1)
                if j == 0 and h == 0:
                    pe.wait_ge(m_in, 32 * (u + 1))
                q0 = diag(u, j)
                sl = (piece0[u] + j // TPC) % KSLOTS
                b = j % TPC * P
                ins = pe.matmul(pS[:, n % SBANKS, q0:CH], kst[0:R_END, sl, h, b:b + P],
                                qst[0:R_END, u % QSLOTS, h, q0:CH], start=True, stop=not is_diag(u, j))
                if is_diag(u, j):
                    ins = pe.matmul(pS[:, n % SBANKS, q0:q0 + P], identb[:, :], maskb[:, :], start=False, stop=True)
                ins.then_inc(scores_ready, 1)

            def weighted(s):
                u, j = steps[s]
                q0 = diag(u, j)
                if j == 0 and u >= 1:
                    pe.wait_ge(ctx_saved, u)
                for h in range(G):
                    pe.wait_ge(probs_ready, G * s + h + 1)
                    pe.matmul(pO[32 * h:32 * h + VW, q0:CH], vals[:, j, units[u][1] * G + h, :],
                              probs[:, (G * s + h) % PSLOTS, q0:CH], start=j == 0, stop=j == n_steps[u] - 1)\
                        .then_inc(pv_done, 1)

            pe.wait_ge(const_ok, 1)
            pe.wait_ge(w_in, 128)
            for g in head_groups:
                side_group(g)
            for k in range(n_turns(0)):
                max_turn(0, k)
            swap_max(0)
            pe.wait_ge(rows_ok, 1)
            for g in head_groups:
                need_empty(pe, g)
            for s, (u, j) in enumerate(steps):
                for h in range(G):
                    scores(s, h)
                    for use in turns_after(s, h):
                        max_turn(*use)
                    if h == 1 and side[s]:
                        side_group(side[s])
                    if h == 2 and s:
                        weighted(s - 1)
                if step_swap[s]:
                    swap_max(step_swap[s])
            weighted(NS - 1)
            pe.wait_ge(probs_ready, G * NS)
            for g in tail_groups:
                side_group(g)

        @block.vector
        def _(dve):
            chain = [0]

            def link(ins):
                chain[0] += 1
                ins.then_inc(vself, 1)
                dve.wait_ge(vself, chain[0])

            def variances(src, t0, t1):
                for t in range(t0, t1):
                    ins = nc.vector.bn_stats(st[:, t, :], src[:, t, :])
                link(ins)
                for t in range(t0, t1):
                    ins = nc.vector.bn_aggr(mv[:, t, :], st[:, t, :])
                link(ins)

            def var_eps():
                nc.vector.tensor_scalar(ve[:, :], mv[:, :, 1], EPS, None, ALU.add).then_inc(var_ok, 1)

            def normalise(dst, src, n):
                dve.wait_ge(rstd_ok, n)
                for t in range(TPC):
                    ins = nc.vector.tensor_scalar(dst[:, t, :], src[:, t, :], mv[:, t, 0:1], rstd[:, t:t + 1],
                                                  ALU.subtract, ALU.mult)
                return ins

            def side_op(g):
                kind = g[0]
                if kind == "v":
                    need_side(dve, g)
                    t0 = g[1] * TPC + 2 * g[2]
                    for t in range(2):
                        ins = nc.vector.tensor_tensor(vals[:, t0 + t, :, 0:HD],
                                                      bank(g)[:, t * D:(t + 1) * D].rearrange("p (h d) -> p h d", h=H),
                                                      bv_b[:, :].rearrange("p (h d) -> p h d", h=H), ALU.add)
                    ins.then_inc(side_v, 1)
                elif kind == "w":
                    need_side(dve, g)
                    if g[1] < 2:
                        dst, n = (w1T, w2T)[g[1]][:, g[2], :], FH
                        nc.vector.tensor_scalar(dst, bank(g).bitcast(BF16)[:, 0:n], -1.0, None, ALU.add)\
                            .then_inc(side_v, 1)
                    else:
                        a = 3 * g[2]
                        full = 3 if g[2] == 0 else 2
                        src = bank(g).bitcast(BF16)[:, 0:3 * D].rearrange("p (t n) -> p t n", t=3)
                        ins = nc.vector.tensor_scalar(w3T[:, a:a + full, :], src[:, 0:full, :], -1.0, None, ALU.add)
                        if full == 2:
                            r = FROWS[FT - 1]
                            ins = nc.vector.tensor_scalar(w3T[0:r, FT - 1, :], src[0:r, 2, :], -1.0, None, ALU.add)
                        ins.then_inc(side_v, 1)
                elif kind == "wo":
                    need_side(dve, g)
                    if g[2] == 0:
                        dve.wait_ge(xb_ok, TPC * (g[1] + 1))
                    t0 = 2 * g[2]
                    rows = x1_of(g[1])
                    nc.vector.tensor_tensor(rows[:, t0:t0 + 2, :], bank(g).rearrange("p (t n) -> p t n", t=2),
                                            rows[:, t0:t0 + 2, :], ALU.add).then_inc(side_v, 1)
                    need_empty(dve, g)
                    variances(rows, t0, t0 + 2)
                    if g[2] == 1:
                        var_eps()
                elif kind == "x2T":
                    dve.wait_ge(half_a, half_no[g] + 1)
                    nc.vector.tensor_tensor(x2T[:, 1, :, :], bank(g).rearrange("p (k n) -> p k n", k=KT),
                                            x2T[:, 0, :, :].bitcast(F32), ALU.subtract).then_inc(side_v, 1)
                elif kind == "up":
                    i, m, rows = up_no[g], g[3], FROWS[g[3]]
                    dve.wait_ge(half_a, half_no[g] + 1)
                    if i >= 2:
                        dve.wait_ge(lo_ok, i - 1)
                    nc.vector.scalar_tensor_tensor(out=hid[0:rows, i % 2, :], in0=th[0:rows, i % 2, :], scalar=1.0,
                                                   in1=bank(g)[0:rows, HALF:CH], op0=ALU.add, op1=ALU.mult)\
                        .then_inc(side_v, 1)
                    need_empty(dve, g)
                    if m == 0 and i >= FT:
                        prev = ups[i - 1]
                        need_side(dve, ("down", prev[1], prev[2]))
                    nc.vector.tensor_copy(hT[0:rows, 0, m, :], hid[0:rows, i % 2, :]).then_inc(hid_ok, 1)
                elif kind == "back":
                    need_side(dve, g)
                    n = 2 * g[1] + g[2]
                    if n:
                        dve.wait_ge(out_done, 16 * n)
                    nc.vector.tensor_tensor(fin, bank(g).rearrange("p (t n) -> p t n", t=2),
                                            x1_of(g[1])[:, 2 * g[2]:2 * g[2] + 2, :], ALU.add).then_inc(side_v, 1)

            def max_turn(u, k):
                i, h, t = turn_of(u, k)
                x = ("turn", u, k)
                bank = max_bank(x)
                if k == 0 and u >= 2:
                    dve.wait_ge(nm_ok, u - 1)
                dve.wait_ge(max_ready, use_no[x] + 1)
                dst = pm[:, u % 2, h * TPC + t, i:i + 1]
                if i < units[u][0]:
                    nc.vector.tensor_reduce(dst, bank, AX.X, ALU.max).then_inc(max_free, 1)
                else:
                    sc = bank[:, 0:(t + 1) * P]
                    nc.vector.tensor_tensor_reduce(out=sc, in0=sc, in1=mask[:, CH - (t + 1) * P:CH], scale=1.0,
                                                   scalar=NEG, op0=ALU.add, op1=ALU.max, accum_out=dst)\
                        .then_inc(max_free, 1)

            def negate(u):
                dve.wait_ge(max_free, turns_to[use_no[("turn", u, n_turns(u) - 1)] + 1])
                if u >= 1:
                    dve.wait_ge(max_ready, use_no[("swap", u - 1)] + 1)
                nc.vector.tensor_reduce(nm[:, :], pm[:, u % 2, :, 0:units[u][0] + 1], AX.X, ALU.max, negate=True)\
                    .then_inc(nm_ok, 1)

            def split_max(u):
                x = ("swap", u)
                dve.wait_ge(max_ready, use_no[x] + 1)
                if u >= 1:
                    dve.wait_ge(m_in, 32 * u)
                m = max_bank(x)[0:G * TPC, 0:P]
                link(nc.vector.tensor_copy(mT[:, 0, :].bitcast(F32R), m))
                nc.vector.tensor_tensor(mT[:, 1, :].bitcast(F32R), m, mT[:, 0, :], ALU.subtract).then_inc(mT_ok, 1)

            def invert(c):
                dve.wait_ge(den_in, 16 * (c + 1))
                nc.vector.reciprocal(dens[:, :], dens[:, :]).then_inc(rden_ok, 1)

            def norm_ctx(c):
                dve.wait_ge(ctx_in, 16 * 2 * KT * (c + 1))
                nc.vector.tensor_tensor(ctx_c, ctx_c, den_c, ALU.mult).then_inc(ctx_ok, 1)

            dve.wait_ge(al_in, 16)
            link(nc.vector.tensor_copy(al[:, 1, :].bitcast(F32R), al[:, 0, :]))
            link(nc.vector.tensor_tensor(al[:, 2, :].bitcast(F32R), al[:, 0, :], al[:, 1, :], ALU.subtract))
            dve.wait_ge(x_in, 16)
            variances(xin, 0, TPC)
            var_eps()
            normalise(xin, xin, 1).then_inc(xn_ok, 1)
            nc.vector.memset(pO[:, :], 0.0)
            nc.vector.memset(vals[:, :, :, HD:VW], 1.0).then_inc(rows_ok, 1)
            dve.wait_ge(w_in, 128)
            need_side(dve, ("xT", 0, KT - 1))
            dve.wait_ge(x_in, 32)
            variances(xin, 0, TPC)
            var_eps()
            normalise(xin, xin, 2).then_inc(xn_ok, 1)
            g = ("gamma",)
            need_side(dve, g)
            link(nc.vector.tensor_scalar(thr[:, 1, 0:3], bank(g)[:, 0:3], 1.0 / (FH * D), QEPS, ALU.mult, ALU.add))
            link(nc.vector.tensor_scalar(thr[:, 0, 0:3], thr[:, 1, 0:3], 0.5, None, ALU.mult))
            nc.vector.tensor_scalar(thr[:, 1, 0:3], thr[:, 0, 0:3], -1.0, None, ALU.mult).then_inc(side_v, 1)
            need_empty(dve, g)
            for i in range(3):
                link(nc.vector.tensor_scalar(tern_v[i], w_rows[i], thr[:, 0, i:i + 1], None, ALU.is_gt))
                nc.vector.scalar_tensor_tensor(out=tern_v[i], in0=w_rows[i], scalar=thr[:, 1, i:i + 1],
                                               in1=tern_v[i], op0=ALU.is_ge, op1=ALU.add).then_inc(tern_ok, 1)
            for g in head_groups:
                if g[0] == "v":
                    side_op(g)
            for k in range(n_turns(0)):
                max_turn(0, k)
            negate(0)
            split_max(0)
            rstds = 2
            for s, (u, j) in enumerate(steps):
                c = units[u][0]
                ph = s - phase0[c]
                for use in step_turns[s]:
                    max_turn(*use)
                if step_swap[s]:
                    split_max(step_swap[s])
                if side[s]:
                    side_op(side[s])
                if ph == 4 and c >= 1:
                    invert(c - 1)
                if ph == 7 and c >= 1:
                    norm_ctx(c - 1)
                if c >= 1 and ph == POST_AT[c] + 3:
                    rstds += 1
                    normalise(xn2, x1, rstds).then_inc(xn2_ok, 1)
                if ph == LN_AT[c]:
                    dve.wait_ge(x_in, 16 * (c + 3))
                    variances(xin, 0, TPC)
                    var_eps()
                if ph == LN_AT[c] + 2:
                    rstds += 1
                    normalise(xin, xin, rstds).then_inc(xn_ok, 1)
                if s + 1 < NS and step_swap[s + 1]:
                    negate(step_swap[s + 1])
            for i, g in enumerate(tail_groups):
                if i == 4:
                    invert(NCH - 1)
                if g == ("wo", NCH - 1, 0):
                    norm_ctx(NCH - 1)
                side_op(g)
                if g == ("wo", NCH - 1, 1):
                    rstds += 1
                    normalise(xn2, x1_of(NCH - 1), rstds).then_inc(xn2_ok, 1)


_INS = ["L0_attn_x", "L0_attn_Wq", "L0_attn_bq", "L0_attn_Wk", "L0_attn_bk", "L0_attn_Wv", "L0_attn_bv",
        "L0_attn_Wo", "L0_attn_bo", "L0_ffn_w1", "L0_ffn_w2", "L0_ffn_w3"]


def _alibi_table(heads, tokens):
    import numpy as np
    ratio = np.float32(2.0 ** (-8.0 / heads))
    slopes = ratio ** np.arange(1, heads + 1, dtype=np.float32)
    distances = np.arange(1 - tokens, 1, dtype=np.float32)
    return (slopes[:, None] * distances[None, :]).astype(np.float32).reshape(128, -1)


def kernel(**inputs):
    import numpy as _np
    import concourse.bacc as _bacc
    from concourse import mybir as _mybir
    from concourse.bass_utils import run_bass_kernel_spmd as _run

    nc = _bacc.Bacc("TRN2", target_bir_lowering=False, num_devices=1)
    arrays, args = {}, []
    for name in _INS:
        a = _np.ascontiguousarray(inputs[name])
        arrays[f"in_{name}"] = a
        args.append(nc.dram_tensor(f"in_{name}", a.shape, _mybir.dt.from_np(a.dtype), kind="ExternalInput").ap())
    table = _alibi_table(16, inputs["L0_attn_x"].shape[1])
    arrays["alibi"] = table
    args.append(nc.dram_tensor("alibi", table.shape, _mybir.dt.float32, kind="ExternalInput").ap())
    shape = inputs["L0_attn_x"].shape
    args.append(nc.dram_tensor("out_0", shape, _mybir.dt.float32, kind="ExternalOutput").ap())
    preln_layer(nc, *args)
    r = _run(nc, [arrays], core_ids=[0])
    return r.results[0]["out_0"]
```

```python
import concourse.bass as bass
from concourse import mybir
from contextlib import ExitStack



def preln_layer(nc, x, Wq, bq, Wk, bk, Wv, bv, Wo, bo, w1, w2, w3, alibi, out):
    F32, F32R, BF16 = mybir.dt.float32, mybir.dt.float32r, mybir.dt.bfloat16
    ALU = mybir.AluOpType
    ACT = mybir.ActivationFunctionType
    AX = mybir.AxisListType

    _, T, D = x.shape
    FH = w1.shape[0]
    H = 16
    HD = D // H
    P = 128
    CH = 512
    NCH = T // CH
    TPC = CH // P
    G = 4
    NHG = H // G
    KT = D // P
    FT = (FH + P - 1) // P
    FROWS = [min(P, FH - i * P) for i in range(FT)]
    HALF = CH // 2
    EPS = 1e-5
    QEPS = 1e-8
    NEG = -3.0e38
    VW = HD + 1
    R_ALIBI = 4 * HD
    R_MAX = 96
    R_END = R_MAX + 2
    KSLOTS, QSLOTS, PSLOTS = 8, 3, 7
    SBANKS, MBANKS = 3, 3
    K_DMAS, Q_DMAS, PART_DMAS = 2, 3, 2 * (P // (G * HD))

    units = [(c, hg) for c in range(NCH) for hg in range(NHG)]
    NU = len(units)
    n_steps = [TPC * (c + 1) for c, _ in units]
    first_step = [sum(n_steps[:u]) for u in range(NU + 1)]
    NS = first_step[NU]
    phase0 = [first_step[c * NHG] for c in range(NCH)] + [NS]
    steps = [(u, j) for u in range(NU) for j in range(n_steps[u])]

    piece0 = [sum(units[v][0] + 1 for v in range(u)) for u in range(NU + 1)]
    pieces = [(u, i) for u in range(NU) for i in range(units[u][0] + 1)]

    def n_turns(u):
        return G * TPC * (units[u][0] + 1)

    def turn_of(u, k):
        return k // (G * TPC), k // TPC % G, k % TPC

    def swap_step(u):
        v = u - 1
        return first_step[u] - (3 if n_steps[v] > TPC else 2)

    LOADS_AT, TURNS_AT = 7, 9

    def turns_start(u):
        s0 = swap_step(u - 1) if u >= 2 else 0
        c, hg = units[u]
        return max(s0, phase0[c - 1] + TURNS_AT) if hg == 0 and c >= 1 else s0

    step_turns = [[] for _ in range(NS)]
    step_swap = [None] * NS
    for u in range(1, NU):
        a, b = turns_start(u), swap_step(u)
        for s in range(a, b):
            step_turns[s] += [(u, k) for k in range(n_turns(u) * (s - a) // (b - a),
                                                     n_turns(u) * (s - a + 1) // (b - a))]
        step_swap[b] = u
    def turns_after(s, h):
        t = step_turns[s]
        return t[(len(t) * h + G - 1) // G:(len(t) * (h + 1) + G - 1) // G]

    bank_use = [("turn", 0, k) for k in range(n_turns(0))] + [("swap", 0)]
    for s in range(NS):
        bank_use += [("turn", *use) for use in step_turns[s]]
        bank_use += [("swap", step_swap[s])] if step_swap[s] else []
    use_no = {x: i for i, x in enumerate(bank_use)}
    turns_to = [0]
    for use in bank_use:
        turns_to.append(turns_to[-1] + (use[0] == "turn"))

    def pre_groups(c):
        return ([("xT", c, k) for k in range(KT)] + [(w, c, m) for m in range(KT) for w in "kq"]
                + [("v", c, i) for i in range(TPC // 2)])

    weight_groups = [("w", i, k) for i in range(3) for k in range(2)]

    def post_groups(c):
        up = [[("up", c, h, m) for m in range(FT)] for h in range(2)]
        if c == NCH - 1:
            return ([("wo", c, 0), ("wo", c, 1), ("x2T", c, 0)] + up[0][:2] + [("x2T", c, 1)] + up[0][2:]
                    + up[1][:2] + [("down", c, 0)] + up[1][2:] + [("down", c, 1)])
        return ([("wo", c, 0), ("wo", c, 1), None, None, ("x2T", c, 0)] + up[0]
                + [("x2T", c, 1), ("down", c, 0)] + up[1] + [None, None, ("down", c, 1)])

    POST_AT = [None, 8, 8, 42]
    late = [("up", NCH - 2, 1, FT - 2), ("up", NCH - 2, 1, FT - 1), ("down", NCH - 2, 1)]
    side = [None] * NS
    for c in range(NCH):
        lst = pre_groups(c + 1) if c + 1 < NCH else []
        lst = lst + (weight_groups if c == 0 else [None] * (POST_AT[c] - len(lst)) + post_groups(c - 1))
        for i, g in enumerate(lst):
            if g and g not in late:
                side[phase0[c] + i] = g
    head_groups = pre_groups(0) + [("gamma",)]
    post = post_groups(NCH - 1)
    tail_groups = [("ctxT",), late[0], ("ctxB",), late[1], *post[0:2], late[2], *post[2:]]
    order = head_groups + [g for g in side if g] + tail_groups
    number = {g: i for i, g in enumerate(order)}
    READS_LAST = {"gamma": "v", "ctxT": "v", "ctxB": "a", "xT": "a", "k": "a", "q": "a", "v": "v", "w": "v", "wo": "v",
                  "x2T": "v", "up": "v", "down": "v"}
    NHEAD, NTAIL0 = len(head_groups), len(order) - len(tail_groups)
    bank_of, prev_user, emptied = [], [], []
    last = {}
    for i, g in enumerate(order):
        b = i % (1 + SBANKS) if i < NHEAD else (i - NTAIL0) % (1 + SBANKS) if i >= NTAIL0 else 0
        bank_of.append(b)
        prev_user.append(last.get(b))
        last[b] = i
        e = READS_LAST[g[0]]
        emptied.append((e, 1 + sum(READS_LAST[q[0]] == e for q in order[:i])))
    LN_AT = {0: 10, 1: 20, 2: -9, 3: -9}
    splits = [g for g in order if g[0] in "kq"]
    split_no = {g: i for i, g in enumerate(splits)}
    halves = [g for g in order if g[0] in ("x2T", "up")]
    half_no = {g: i for i, g in enumerate(halves)}
    TERN_STEPS = range(0, 6)
    ups = [g for g in order if g[0] == "up"]
    up_no = {g: i for i, g in enumerate(ups)}

    parts = nc.dram_tensor("parts", (2, NCH, NHG, 2, HD, G, CH), F32, kind="Internal").ap()
    alibi_parts = nc.dram_tensor("alibi_parts", (2, H, T), F32, kind="Internal").ap()
    rden_dram = nc.dram_tensor("rden_dram", (NCH, H, CH), F32, kind="Internal").ap()
    ctx_dram = nc.dram_tensor("ctx_dram", (NCH, NHG, G, 32, CH), F32, kind="Internal").ap()

    es = ExitStack()
    with es:
        def sb(name, shape, dt=F32):
            return es.enter_context(nc.sbuf_tensor(name, shape, dt))

        def sem(name):
            return es.enter_context(nc.semaphore(name))

        kst = sb("kst", [P, KSLOTS, G, CH], F32R)
        qst = sb("qst", [P, QSLOTS, G, CH], F32R)
        probs = sb("probs", [P, PSLOTS, CH])
        vals = sb("vals", [P, T // P, H, VW])
        xin = sb("xin", [P, TPC, D])
        xnT = sb("xnT", [P, KT, CH])
        wq_s, wk_s, wv_s, wo_s = (sb(n, [P, KT, D]) for n in ("wq_s", "wk_s", "wv_s", "wo_s"))
        w1T, w2T = sb("w1T", [P, KT, FH], F32R), sb("w2T", [P, KT, FH], F32R)
        w3T = sb("w3T", [P, FT, D], F32R)
        qk_f = sb("qk_f", [P, CH])
        qk_hl = sb("qk_hl", [P, 2, 2, CH])
        ctx_raw = sb("ctx_raw", [P, CH])
        work = sb("work", [P, 5120])
        ctx_c = work[:, 0:1024].rearrange("p (m n) -> p m n", m=KT)
        den_c = work[:, 1024:2048].rearrange("p (m n) -> p m n", m=KT)
        xn2 = work[:, 1024:2048].rearrange("p (t n) -> p t n", t=TPC)
        x1 = work[:, 2048:3072].rearrange("p (t n) -> p t n", t=TPC)
        ctx_n = qk_f[:, :].rearrange("p (t n) -> p t n", t=TPC)
        th = work[:, 3072:3584].rearrange("p (i n) -> p i n", i=2)
        hid = work[:, 3584:4096].rearrange("p (i n) -> p i n", i=2)
        fin = work[:, 4608:5120].rearrange("p (t n) -> p t n", t=2)
        w_at = [0, KT * FH + KT * FH // 2 + FT * D // 2]
        w_rows = [vals[:, T // P // 2:T // P, :, :].rearrange("p t h w -> p (t h w)")[:, 0:FT * D]
                  .rearrange("p (t n) -> p t n", n=D),
                  work[:, w_at[1]:w_at[1] + FT * D].rearrange("p (t n) -> p t n", n=D),
                  work[:, 0:KT * FH].rearrange("p (t n) -> p t n", n=FH)]
        t_at = [0, KT * FH, KT * FH + FT * D // 2]
        tern_v = [work[:, t_at[0]:t_at[0] + FT * D // 2].bitcast(BF16).rearrange("p (t n) -> p t n", n=D),
                  work[:, t_at[1]:t_at[1] + FT * D // 2].bitcast(BF16).rearrange("p (t n) -> p t n", n=D),
                  work[:, t_at[2]:t_at[2] + KT * FH // 2].bitcast(BF16).rearrange("p (t n) -> p t n", n=FH)]
        flat = probs[:, :, :].rearrange("p a n -> p (a n)")
        al = flat[:, 4 * CH:4 * CH + 3 * H * T // P].rearrange("p (a n) -> p a n", a=3)
        ones = flat[:, 6 * CH:6 * CH + P]
        w_abs = flat[:, 0:FT * D]
        x2T = sb("x2T", [P, 2, KT, HALF], F32R)
        hT = sb("hT", [P, 2, FT, HALF], F32R)
        mask = sb("mask", [P, CH], BF16)
        maskb = sb("maskb", [P, P], BF16)
        ident = sb("ident", [P, P])
        identb = sb("identb", [P, P], BF16)
        bias_q, bias_k = sb("bias_q", [P, KT]), sb("bias_k", [P, KT])
        bv_b, bo_b = sb("bv_b", [P, D]), sb("bo_b", [P, D])
        bq_raw = sb("bq_raw", [P, KT])
        wsum = sb("wsum", [P, 4])
        thr = sb("thr", [P, 2, 4])
        rd = sb("rd", [P, TPC * G])
        st = sb("st", [P, TPC, 6])
        mv = sb("mv", [P, TPC, 2])
        ve = sb("ve", [P, TPC])
        mhalf = sb("mhalf", [P, TPC])
        rstd = sb("rstd", [P, TPC])
        pm = sb("pm", [P, 2, G * TPC, NCH])
        nm = sb("nm", [P, G * TPC])
        dens = sb("dens", [P, H * CH // P])
        mT = sb("mT", [G * TPC, 2, P])

        pS = es.enter_context(nc.psum_tensor("pS", [P, SBANKS, CH], F32))
        pO = es.enter_context(nc.psum_tensor("pO", [P, CH], F32))
        pM = es.enter_context(nc.psum_tensor("pM", [P, MBANKS, CH], F32))
        pW = es.enter_context(nc.psum_tensor("pW", [P, CH], F32))

        def x1_of(c):
            return x1 if c < NCH - 1 else xin[:, :, :]

        spare = kst[:, 0:4, :, :].rearrange("p a h n -> p (a h n)")
        x2T_last = spare[:, 0:2 * KT * HALF].rearrange("p (a k n) -> p a k n", a=2, k=KT)
        hT_last = spare[:, 2 * KT * HALF:(2 * KT + 2 * FT) * HALF].rearrange("p (a f n) -> p a f n", a=2, f=FT)

        def x2T_of(g):
            return x2T_last if g[1:3] == (NCH - 1, 1) else x2T[:, :, :, :]

        def hT_of(g):
            return hT_last if g[1:3] == (NCH - 1, 1) else hT[:, :, :, :]

        def bank(g):
            b = bank_of[number[g]]
            return pW[:, :] if b == 0 else pS[:, b - 1, :]

        x_in = sem("x_in")
        w_in = sem("w_in")
        raw_in = sem("raw_in")
        al_in = sem("al_in")
        al_out = sem("al_out")
        x1_in = sem("x1_in")
        xlast_in = sem("xlast_in")
        const_ok = sem("const_ok")
        pad_ok = sem("pad_ok")
        rows_ok = sem("rows_ok")
        k_rows = sem("k_rows")
        q_rows = sem("q_rows")
        vself = sem("vself")
        pself = sem("pself")
        var_ok = sem("var_ok")
        rstd_ok = sem("rstd_ok")
        xn_ok = sem("xn_ok")
        xn2_ok = sem("xn2_ok")
        wsum_ok = sem("wsum_ok")
        gt_ok = sem("gt_ok")
        tern_ok = sem("tern_ok")
        side_ready = sem("side_ready")
        side_a = sem("side_a")
        side_v = sem("side_v")
        half_a = sem("half_a")
        split_ok = sem("split_ok")
        parts_out = [sem(f"parts_out{i}") for i in range(2)]
        k_in = [sem(f"k_in{i}") for i in range(KSLOTS)]
        q_in = [sem(f"q_in{i}") for i in range(QSLOTS)]
        m_in = sem("m_in")
        max_ready = sem("max_ready")
        max_free = sem("max_free")
        nm_ok = sem("nm_ok")
        mT_ok = sem("mT_ok")
        scores_ready = sem("scores_ready")
        probs_ready = sem("probs_ready")
        pv_done = sem("pv_done")
        ctx_saved = sem("ctx_saved")
        ctx_out = sem("ctx_out")
        ctx_in = sem("ctx_in")
        den_in = sem("den_in")
        rden_ok = sem("rden_ok")
        rden_out = sem("rden_out")
        ctx_ok = sem("ctx_ok")
        xb_ok = sem("xb_ok")
        hid_ok = sem("hid_ok")
        lo_ok = sem("lo_ok")
        out_done = sem("out_done")

        block = es.enter_context(nc.Block())

        def diag(u, j):
            return max(0, j - TPC * units[u][0]) * P

        def is_diag(u, j):
            return j >= TPC * units[u][0]

        def max_bank(x):
            return pM[:, use_no[x] % MBANKS, :]

        def need_max_bank(eng, x):
            i = use_no[x] - MBANKS
            if i >= 0 and bank_use[i][0] == "turn":
                eng.wait_ge(max_free, turns_to[i + 1])
            elif i >= 0:
                eng.wait_ge(mT_ok, bank_use[i][1] + 1)

        def den_rows(c):
            return P if c < NCH - 1 else P - P // NHG

        def need_side(eng, g):
            eng.wait_ge(side_ready, number[g] + 1)

        def need_empty(eng, g):
            e, n = emptied[number[g]]
            eng.wait_ge(side_a if e == "a" else side_v, n)

        @block.sync
        def _(sp):
            def load_x(c):
                if c >= 1:
                    need_side(sp, ("xT", c - 1, KT - 1))
                sp.dma_start(xin[:, :, :], x[0, c * CH:(c + 1) * CH, :].rearrange("(t p) d -> p t d", p=P))\
                    .then_inc(x_in, 16)

            def load_x1(c):
                if c == 0:
                    need_side(sp, weight_groups[-1])
                elif c < NCH - 1:
                    need_empty(sp, ("down", c - 1, 1))
                else:
                    need_side(sp, ("xT", c, KT - 1))
                sp.dma_start(x1_of(c), x[0, c * CH:(c + 1) * CH, :].rearrange("(t p) d -> p t d", p=P))\
                    .then_inc(x1_in if c < NCH - 1 else xlast_in, 16)

            def store_parts(g):
                i = split_no[g]
                w = 0 if g[0] == "q" else 1
                sp.wait_ge(split_ok, i + 1)
                for part in range(2):
                    for a in range(P // (G * HD)):
                        sp.dma_start(parts[w, g[1], g[2] * (P // (G * HD)) + a, part, :, :, :]
                                     .rearrange("d h n -> h d n"),
                                     qk_hl[a * G * HD:(a + 1) * G * HD, i % 2, part, :])\
                            .then_inc(parts_out[i % 2], 16)

            def parts_there(w, c, hg):
                i = split_no[(w, c, hg * G * HD // P)]
                sp.wait_ge(parts_out[i % 2], PART_DMAS * 16 * (i // 2 + 1))

            def load_k(n):
                v, i = pieces[n]
                parts_there("k", i, units[v][1])
                if n >= KSLOTS:
                    pu, pi = pieces[n - KSLOTS]
                    sp.wait_ge(scores_ready, G * (first_step[pu] + TPC * pi + TPC))
                if n < KSLOTS:
                    sp.wait_ge(k_rows, n + 1)
                hg = units[v][1]
                src = parts[1, i, hg, :, :, :, :].rearrange("(a p) d h n -> a (p d) (h n)", a=1)
                sp.dma_start(kst[0:4 * HD, n % KSLOTS, :, :].bitcast(F32).rearrange("r h n -> r (h n)"),
                             src.to_broadcast([2, 2 * HD, G * CH])).then_inc(k_in[n % KSLOTS], 16)
                sp.dma_start(kst[R_ALIBI:R_ALIBI + 2, n % KSLOTS, :, :].bitcast(F32),
                             alibi_parts[:, hg * G:(hg + 1) * G, i * CH:(i + 1) * CH])\
                    .then_inc(k_in[n % KSLOTS], 16)

            def load_q(v):
                c, hg = units[v]
                parts_there("q", c, hg)
                if v >= QSLOTS:
                    sp.wait_ge(scores_ready, G * first_step[v - QSLOTS + 1])
                if v < QSLOTS:
                    sp.wait_ge(q_rows, v + 1)
                src = parts[0, c, hg, :, :, :, :]
                dst = qst[:, v % QSLOTS, :, :].bitcast(F32).rearrange("r h n -> r (h n)")
                sp.dma_start(dst[0:2 * HD, :], src.rearrange("p d h n -> (p d) (h n)"))\
                    .then_inc(q_in[v % QSLOTS], 16)
                for b in range(2):
                    sp.dma_start(dst[(2 + b) * HD:(3 + b) * HD, :],
                                 src[1 - b, :, :, :].rearrange("d h n -> d (h n)"))\
                        .then_inc(q_in[v % QSLOTS], 16)

            def load_m(v):
                sp.wait_ge(mT_ok, v + 1)
                for part in range(2):
                    sp.dma_start(qst[R_MAX + part:R_MAX + part + 1, v % QSLOTS, :, :].bitcast(F32)
                                 .rearrange("o h (t n) -> o (h t) n", n=P),
                                 mT[:, part, :]).then_inc(m_in, 16)

            def store_ctx(u):
                sp.wait_ge(ctx_saved, u + 1)
                c, hg = units[u]
                sp.dma_start(ctx_dram[c, hg, :, :, :].rearrange("h r n -> (h r) n"), ctx_raw[:, :])\
                    .then_inc(ctx_out, 16)

            def ctx_rows(c, m):
                return P if c < NCH - 1 or m < KT - 1 else P - G * HD

            def load_ctx(c):
                sp.wait_ge(ctx_out, 16 * (NHG * (c + 1) - (c == NCH - 1)))
                need_side(sp, ("wo", c - 1, 1) if c >= 1 else weight_groups[-1])
                by_head = ctx_dram[c, :, :, :, :].rearrange("g h r n -> (g h) r n")
                n = den_rows(c)
                sp.dma_start(dens[0:n, :], by_head[0:n * H // P, HD, :].rearrange("h (i n) -> h i n", i=P // H))\
                    .then_inc(den_in, 16)
                for m in range(KT):
                    r, h0 = ctx_rows(c, m), m * P // HD
                    sp.dma_start(ctx_c[0:r, m, :], by_head[h0:h0 + r // HD, 0:HD, :])\
                        .then_inc(ctx_in, 16)

            def spread_rden(c):
                sp.wait_ge(rden_ok, c + 1)
                n = den_rows(c)
                sp.dma_start(rden_dram[c, 0:n * H // P, :].rearrange("h (i n) -> (h i) n", i=P // H), dens[0:n, :])\
                    .then_inc(rden_out, 16)
                sp.wait_ge(rden_out, 16 * (c + 1))
                if c >= 1:
                    need_side(sp, ("x2T", c - 1, 1))
                for m in range(KT):
                    r, h0 = ctx_rows(c, m), m * P // HD
                    rows = rden_dram[c, h0:h0 + r // HD, :].rearrange("h (a n) -> h a n", a=1)
                    sp.dma_start(den_c[0:r, m, :], rows.to_broadcast([r // HD, HD, CH])).then_inc(ctx_in, 16)

            def store_out(c, h):
                need_empty(sp, ("down", c, h))
                t0 = c * CH + h * HALF
                sp.dma_start(out[0, t0:t0 + HALF, :].rearrange("(t p) d -> p t d", p=P), fin)\
                    .then_inc(out_done, 16)

            load_x(0)
            sp.dma_start(al[:, 0, :], alibi).then_inc(al_in, 16)
            for dst, src in ((wk_s, Wk), (wq_s, Wq), (wv_s, Wv), (wo_s, Wo)):
                sp.dma_start(dst[:, :, :], src.rearrange("(k p) n -> p k n", p=P)).then_inc(w_in, 16)
            for dst, src in ((bq_raw, bq), (bias_k, bk)):
                sp.dma_start(dst[:, :], src.rearrange("(m p) -> p m", p=P), allow_slow_non_contiguous=True)\
                    .then_inc(w_in, 16)
            for dst, src in ((bv_b, bv), (bo_b, bo)):
                sp.dma_start(dst[:, :], src.rearrange("(a n) -> a n", a=1).to_broadcast([P, D]))\
                    .then_inc(w_in, 16)
            sp.wait_ge(pad_ok, 1)
            FF = (FT - 1) * P
            for i, w in enumerate((w1, w2)):
                sp.dma_start(w_rows[i][:, 0:FT - 1, :], w[0:FF, :].rearrange("(t p) n -> p t n", p=P))\
                    .then_inc(raw_in, 16)
                sp.dma_start(w_rows[i][0:FH - FF, FT - 1, :], w[FF:FH, :]).then_inc(raw_in, 16)
            sp.dma_start(w_rows[2], w3.rearrange("(t p) n -> p t n", p=P)).then_inc(raw_in, 16)
            sp.wait_ge(vself, 2)
            for part in range(2):
                sp.dma_start(alibi_parts[part, :, :].rearrange("h (i n) -> (h i) n", n=H * T // P),
                             al[:, 1 + part, :]).then_inc(al_out, 16)
            load_x(1)
            sp.wait_ge(al_out, 32)
            store_parts(("k", 0, 0))
            store_parts(("q", 0, 0))
            load_k(0)
            load_q(0)
            store_parts(("k", 0, 1))
            store_parts(("q", 0, 1))
            load_k(1)
            load_q(1)
            load_m(0)

            k_at, q_at = {}, {}
            for n in range(2, len(pieces)):
                v, i = pieces[n]
                c = units[v][0]
                s = 0
                if n >= KSLOTS:
                    pu, pi = pieces[n - KSLOTS]
                    s = first_step[pu] + TPC * pi + TPC - 1
                if c >= 1:
                    s = max(s, phase0[c - 1] + LOADS_AT)
                k_at.setdefault(s, []).append(n)
            for v in range(2, NU):
                c = units[v][0]
                s = first_step[v - QSLOTS + 1] - 1 if v >= QSLOTS else 0
                if c >= 1:
                    s = max(s, phase0[c - 1] + LOADS_AT)
                q_at.setdefault(s, []).append(v)
            for s, (u, j) in enumerate(steps):
                c, hg = units[u]
                ph = s - phase0[c]
                g = side[s - 1] if s else None
                if g and g[0] in "kq":
                    store_parts(g)
                if g and g[0] == "down":
                    store_out(g[1], g[2])
                for n in k_at.get(s, []):
                    load_k(n)
                for v in q_at.get(s, []):
                    load_q(v)
                if step_swap[s]:
                    load_m(step_swap[s])
                if j == 0 and u >= 1:
                    store_ctx(u - 1)
                if ph == 1 and c >= 1:
                    load_ctx(c - 1)
                    load_x1(c - 1)
                    if c == NCH - 1:
                        load_x1(c)
                if ph == 3 and c + 2 < NCH:
                    load_x(c + 2)
                if ph == 4 and c >= 1:
                    spread_rden(c - 1)
                if u == NU - 1 and j == 1:
                    load_ctx(c)
                if u == NU - 1 and j == 6:
                    spread_rden(c)
            for g in tail_groups:
                if g[0] == "down":
                    store_out(g[1], g[2])
            sp.wait_ge(out_done, 16 * 2 * NCH)

        @block.gpsimd
        def _(pool):
            chain = [0]

            def link(ins):
                chain[0] += 1
                ins.then_inc(pself, 1)
                pool.wait_ge(pself, chain[0])

            link(nc.gpsimd.memset(mhalf[:, :], -0.5))
            for i in range(2):
                ins = nc.gpsimd.memset(w_rows[i][FROWS[FT - 1]:P, FT - 1, :], 0.0)
            ins.then_inc(pad_ok, 1)
            pool.wait_ge(pad_ok, 1)
            link(nc.gpsimd.memset(ident[:, :], 0.0))
            link(nc.gpsimd.affine_select(out=ident[:, :], in_=ident[:, :], compare_op=ALU.not_equal, fill=1.0,
                                         base=0, pattern=[[-1, P]], channel_multiplier=1))
            link(nc.gpsimd.tensor_copy(identb[:, :], ident[:, :]))
            link(nc.gpsimd.memset(mask[:, :], 0.0))
            link(nc.gpsimd.affine_select(out=mask[:, CH - P:CH], in_=mask[:, CH - P:CH], compare_op=ALU.is_ge,
                                         fill=NEG, base=0, pattern=[[-1, P]], channel_multiplier=1))
            link(nc.gpsimd.memset(maskb[:, :], 0.0))
            link(nc.gpsimd.affine_select(out=maskb[:, :], in_=maskb[:, :], compare_op=ALU.is_ge, fill=NEG,
                                         base=0, pattern=[[1, P]], channel_multiplier=-1))
            nc.gpsimd.memset(ones, 1.0).then_inc(const_ok, 1)

            pool.wait_ge(const_ok, 1)

            def power(n, t0=0, t1=TPC):
                pool.wait_ge(var_ok, n)
                nc.gpsimd.tensor_tensor(rstd[:, t0:t1], ve[:, t0:t1], mhalf[:, t0:t1], ALU.pow).then_inc(rstd_ok, 1)
                pool.wait_ge(rstd_ok, n)

            def add_bo(c):
                if c < NCH - 1:
                    pool.wait_ge(x1_in, 16 * (c + 1))
                else:
                    pool.wait_ge(xlast_in, 16)
                for t in range(TPC):
                    ins = nc.gpsimd.tensor_tensor(x1_of(c)[:, t, :], x1_of(c)[:, t, :], bo_b[:, :], ALU.add)
                    ins.then_inc(xb_ok, 1)
                    pool.wait_ge(xb_ok, TPC * c + t + 1)

            def lo_part(g):
                i, m, rows = up_no[g], g[3], FROWS[g[3]]
                pool.wait_ge(hid_ok, i + 1)
                nc.gpsimd.tensor_tensor(hT_of(g)[0:rows, 1, m, :], hid[0:rows, i % 2, :],
                                        hT_of(g)[0:rows, 0, m, :].bitcast(F32), ALU.subtract).then_inc(lo_ok, 1)
                pool.wait_ge(lo_ok, i + 1)

            def key_rows(n):
                nc.gpsimd.memset(kst[R_ALIBI:R_END, n, :, :].bitcast(F32), 1.0).then_inc(k_rows, 1)
                pool.wait_ge(k_rows, n + 1)

            def query_rows(n):
                link(nc.gpsimd.memset(qst[R_ALIBI:R_MAX, n, :, :].bitcast(F32), 0.0))
                nc.gpsimd.memset(qst[R_ALIBI:R_ALIBI + 2, n, :, :].bitcast(F32), 1.0).then_inc(q_rows, 1)
                pool.wait_ge(q_rows, n + 1)

            def split_lo(g):
                i = split_no[g]
                need_empty(pool, g)
                hi, lo = qk_hl[:, i % 2, 0, :], qk_hl[:, i % 2, 1, :]
                nc.gpsimd.tensor_tensor(lo.bitcast(F32R), qk_f[:, :], hi, ALU.subtract).then_inc(split_ok, 1)
                pool.wait_ge(split_ok, i + 1)

            key_rows(0)
            power(1)
            query_rows(0)
            split_lo(("k", 0, 0))
            split_lo(("q", 0, 0))
            power(2)
            split_lo(("k", 0, 1))
            split_lo(("q", 0, 1))
            for n in range(1, QSLOTS):
                key_rows(n)
                query_rows(n)
            for n in range(QSLOTS, KSLOTS):
                key_rows(n)
            powers = 2
            pool.wait_ge(w_in, 128)
            for s, (u, j) in enumerate(steps):
                c = units[u][0]
                ph = s - phase0[c]
                g = side[s]
                if g and g[0] in "kq":
                    split_lo(g)
                if g and g[0] == "up":
                    lo_part(g)
                if ph == 2 and c >= 1:
                    add_bo(c - 1)
                if ph == 2 and c == NCH - 1:
                    add_bo(c)
                if (c >= 1 and ph == POST_AT[c] + 2) or ph == LN_AT[c] + 1:
                    powers += 1
                    power(powers)
            for h in range(2):
                power(powers + 1 + h, 2 * h, 2 * h + 2)

        @block.scalar
        def _(act):
            def side_op(g):
                kind = g[0]
                if kind == "xT":
                    need_side(act, g)
                    if g[1] >= 1:
                        need_side(act, ("v", g[1] - 1, 1))
                    nc.scalar.activation(xnT[:, g[2], :], bank(g), ACT.Copy).then_inc(side_a, 1)
                elif kind in "kq":
                    need_side(act, g)
                    i = split_no[g]
                    if i >= 1:
                        act.wait_ge(split_ok, i)
                    if i >= 2:
                        act.wait_ge(parts_out[i % 2], PART_DMAS * 16 * (i // 2))
                    b, sc = (bias_k, 1.0) if kind == "k" else (bias_q, HD ** -0.5)
                    nc.scalar.activation(qk_f[:, :], bank(g), ACT.Identity, bias=b[:, g[2]:g[2] + 1], scale=sc)
                    nc.scalar.activation(qk_hl[:, i % 2, 0, :].bitcast(F32R), bank(g), ACT.Identity,
                                         bias=b[:, g[2]:g[2] + 1], scale=sc).then_inc(side_a, 1)
                elif kind == "ctxB":
                    need_side(act, g)
                    act.wait_ge(ctx_ok, NCH)
                    nc.scalar.activation(ctx_c[P - G * HD:P, KT - 1, :], bank(g)[P - G * HD:P, :], ACT.Copy)\
                        .then_inc(side_a, 1)
                elif kind == "x2T":
                    need_side(act, g)
                    if g[1] < NCH - 1 and g[2] + g[1] >= 1 or g[1] == NCH - 1 and g[2] == 0:
                        need_side(act, ("up", g[1] - 1 + g[2], 1 - g[2], FT - 1))
                    nc.scalar.activation(x2T_of(g)[:, 0, :, :], bank(g).rearrange("p (k n) -> p k n", k=KT), ACT.Copy)\
                        .then_inc(half_a, 1)
                elif kind == "up":
                    i, rows = up_no[g], FROWS[g[3]]
                    need_side(act, g)
                    if i >= 2:
                        act.wait_ge(hid_ok, i - 1)
                    nc.scalar.activation(th[0:rows, i % 2, :], bank(g)[0:rows, 0:HALF], ACT.Tanh, scale=0.5)\
                        .then_inc(half_a, 1)

            def exps(s, h):
                u, j = steps[s]
                n = G * s + h
                q0 = diag(u, j)
                act.wait_ge(scores_ready, n + 1)
                if n >= PSLOTS:
                    act.wait_ge(pv_done, n - PSLOTS + 1)
                nc.scalar.activation(probs[:, n % PSLOTS, q0:CH], pS[:, n % SBANKS, q0:CH], ACT.Exp)\
                    .then_inc(probs_ready, 1)

            def save_ctx(u):
                act.wait_ge(pv_done, G * first_step[u + 1])
                if u >= 1:
                    act.wait_ge(ctx_out, 16 * u)
                nc.scalar.activation(ctx_raw[:, :], pO[:, :], ACT.Copy).then_inc(ctx_saved, 1)

            act.wait_ge(w_in, 128)
            nc.scalar.mul(bias_q[:, :], bq_raw[:, :], HD ** -0.5).then_inc(wsum_ok, 1)
            act.wait_ge(wsum_ok, 1)
            for g in head_groups:
                if g[0] in ("xT", "k", "q"):
                    side_op(g)
            act.wait_ge(raw_in, 80)
            for i in range(3):
                act.wait_ge(wsum_ok, i + 1)
                wr = w_rows[i].rearrange("p t n -> p (t n)")
                nc.scalar.activation(w_abs[:, 0:wr.shape[1]], wr, ACT.Abs, accum_out=wsum[:, i:i + 1])\
                    .then_inc(wsum_ok, 1)
            for s, (u, j) in enumerate(steps):
                for h in range(G):
                    exps(s, h)
                    if h == 2 and side[s]:
                        side_op(side[s])
                if j == 0 and u >= 1:
                    save_ctx(u - 1)
            save_ctx(NU - 1)
            for g in tail_groups:
                side_op(g)

        @block.tensor
        def _(pe):
            def side_group(g):
                kind = g[0]
                if prev_user[number[g]] is not None:
                    need_empty(pe, order[prev_user[number[g]]])
                w = bank(g)
                if kind == "xT":
                    pe.wait_ge(xn_ok, g[1] + 1)
                    for t in range(TPC):
                        ins = pe.transpose(w[:, t * P:(t + 1) * P], xin[:, t, g[2] * P:(g[2] + 1) * P], ident[:, :])
                elif kind in "kq":
                    need_empty(pe, ("xT", g[1], KT - 1))
                    for k in range(KT):
                        ins = pe.matmul(w, (wk_s if kind == "k" else wq_s)[:, k, g[2] * P:(g[2] + 1) * P],
                                        xnT[:, k, :], start=k == 0, stop=k == KT - 1)
                elif kind == "v":
                    for i in range(2):
                        t = 2 * g[2] + i
                        for k in range(KT):
                            ins = pe.matmul(w[:, i * D:(i + 1) * D], xnT[:, k, t * P:(t + 1) * P], wv_s[:, k, :],
                                            start=k == 0, stop=k == KT - 1)
                elif kind == "gamma":
                    pe.wait_ge(wsum_ok, 4)
                    ins = pe.matmul(w[:, 0:3], ones, wsum[:, 0:3], start=True, stop=True)
                elif kind == "w":
                    wb = w.bitcast(BF16)
                    if g[1] == 0 or g[1] == 1:
                        pe.wait_ge(tern_ok, 3)
                        for t, r in enumerate(FROWS):
                            ins = pe.transpose(wb[:, t * P:t * P + r], tern_v[g[1]][0:r, t, g[2] * P:(g[2] + 1) * P],
                                               identb[0:r, 0:r])
                    else:
                        for i in range(3):
                            f = 3 * g[2] + i
                            r = FROWS[f]
                            for m in range(KT):
                                ins = pe.transpose(wb[0:r, i * D + m * P:i * D + (m + 1) * P],
                                                   tern_v[2][:, m, f * P:f * P + r], identb[:, :])
                elif kind == "ctxT":
                    pe.wait_ge(ctx_saved, NU)
                    for t in range(TPC):
                        ins = pe.transpose(w[:, t * P:(t + 1) * P], ctx_raw[:, t * P:(t + 1) * P], ident[:, :])
                elif kind == "ctxB":
                    need_empty(pe, ("ctxT",))
                    for t in range(TPC):
                        ins = pe.transpose(w[:, t * P:(t + 1) * P], ctx_n[:, t, :], ident[:, :])
                elif kind == "wo":
                    pe.wait_ge(ctx_ok, g[1] + 1)
                    if g[1] == NCH - 1:
                        need_empty(pe, ("ctxB",))
                    for i in range(2):
                        t = 2 * g[2] + i
                        for m in range(KT):
                            ins = pe.matmul(w[:, i * D:(i + 1) * D], ctx_c[:, m, t * P:(t + 1) * P], wo_s[:, m, :],
                                            start=m == 0, stop=m == KT - 1)
                elif kind == "x2T":
                    pe.wait_ge(xn2_ok, g[1] + 1 + (g[2] if g[1] == NCH - 1 else 0))
                    for k in range(KT):
                        for i in range(2):
                            ins = pe.transpose(w[:, k * HALF + i * P:k * HALF + (i + 1) * P],
                                               xn2[:, 2 * g[2] + i, k * P:(k + 1) * P], ident[:, :])
                elif kind == "up":
                    need_empty(pe, ("x2T", g[1], g[2]))
                    m, r = g[3], FROWS[g[3]]
                    for i, wT in enumerate((w1T, w2T)):
                        for k in range(KT):
                            for part in range(2):
                                ins = pe.matmul(w[0:r, i * HALF:(i + 1) * HALF], wT[:, k, m * P:m * P + r],
                                                x2T_of(g)[:, part, k, :], start=k == 0 and part == 0,
                                                stop=k == KT - 1 and part == 1)
                elif kind == "down":
                    for i in range(2):
                        for f, r in enumerate(FROWS):
                            if i == 0:
                                pe.wait_ge(lo_ok, up_no[("up", g[1], g[2], f)] + 1)
                            for part in range(2):
                                ins = pe.matmul(w[:, i * D:(i + 1) * D], hT_of(g)[0:r, part, f, i * P:(i + 1) * P],
                                                w3T[0:r, f, :], start=f == 0 and part == 0,
                                                stop=f == FT - 1 and part == 1)
                ins.then_inc(side_ready, 1)

            def max_turn(u, k):
                i, h, t = turn_of(u, k)
                c = units[u][0]
                if k == 0:
                    pe.wait_ge(q_in[u % QSLOTS], Q_DMAS * 16 * (u // QSLOTS + 1))
                n = piece0[u] + i
                if h == 0 and t == 0:
                    pe.wait_ge(k_in[n % KSLOTS], K_DMAS * 16 * (n // KSLOTS + 1))
                x = ("turn", u, k)
                need_max_bank(pe, x)
                N = CH if i < c else (t + 1) * P
                pe.matmul(max_bank(x)[:, 0:N], qst[0:R_MAX, u % QSLOTS, h, t * P:(t + 1) * P],
                          kst[0:R_MAX, n % KSLOTS, h, 0:N], start=True, stop=True).then_inc(max_ready, 1)

            def swap_max(u):
                x = ("swap", u)
                need_max_bank(pe, x)
                pe.wait_ge(nm_ok, u + 1)
                pe.transpose(max_bank(x)[0:G * TPC, 0:P], nm[:, :], ident[:, :]).then_inc(max_ready, 1)

            def scores(s, h):
                u, j = steps[s]
                n = G * s + h
                if n >= SBANKS:
                    pe.wait_ge(probs_ready, n - SBANKS + 1)
                if j == 0 and h == 0:
                    pe.wait_ge(m_in, 32 * (u + 1))
                q0 = diag(u, j)
                sl = (piece0[u] + j // TPC) % KSLOTS
                b = j % TPC * P
                ins = pe.matmul(pS[:, n % SBANKS, q0:CH], kst[0:R_END, sl, h, b:b + P],
                                qst[0:R_END, u % QSLOTS, h, q0:CH], start=True, stop=not is_diag(u, j))
                if is_diag(u, j):
                    ins = pe.matmul(pS[:, n % SBANKS, q0:q0 + P], identb[:, :], maskb[:, :], start=False, stop=True)
                ins.then_inc(scores_ready, 1)

            def weighted(s):
                u, j = steps[s]
                q0 = diag(u, j)
                if j == 0 and u >= 1:
                    pe.wait_ge(ctx_saved, u)
                for h in range(G):
                    pe.wait_ge(probs_ready, G * s + h + 1)
                    pe.matmul(pO[32 * h:32 * h + VW, q0:CH], vals[:, j, units[u][1] * G + h, :],
                              probs[:, (G * s + h) % PSLOTS, q0:CH], start=j == 0, stop=j == n_steps[u] - 1)\
                        .then_inc(pv_done, 1)

            pe.wait_ge(const_ok, 1)
            pe.wait_ge(w_in, 128)
            for g in head_groups[:-1]:
                side_group(g)
            for k in range(n_turns(0)):
                max_turn(0, k)
            side_group(head_groups[-1])
            swap_max(0)
            pe.wait_ge(rows_ok, 1)
            for g in head_groups[:-1]:
                need_empty(pe, g)
            for s, (u, j) in enumerate(steps):
                for h in range(G):
                    scores(s, h)
                    for use in turns_after(s, h):
                        max_turn(*use)
                    if h == 1 and side[s]:
                        side_group(side[s])
                    if h == 2 and s:
                        weighted(s - 1)
                if step_swap[s]:
                    swap_max(step_swap[s])
            weighted(NS - 1)
            pe.wait_ge(probs_ready, G * NS)
            for g in tail_groups:
                side_group(g)

        @block.vector
        def _(dve):
            chain = [0]

            def link(ins):
                chain[0] += 1
                ins.then_inc(vself, 1)
                dve.wait_ge(vself, chain[0])

            def variances(src, t0, t1):
                for t in range(t0, t1):
                    ins = nc.vector.bn_stats(st[:, t, :], src[:, t, :])
                link(ins)
                for t in range(t0, t1):
                    ins = nc.vector.bn_aggr(mv[:, t, :], st[:, t, :])
                link(ins)

            def var_eps(t0=0, t1=TPC):
                nc.vector.tensor_scalar(ve[:, t0:t1], mv[:, t0:t1, 1], EPS, None, ALU.add).then_inc(var_ok, 1)

            def normalise(dst, src, n, t0=0, t1=TPC):
                dve.wait_ge(rstd_ok, n)
                for t in range(t0, t1):
                    ins = nc.vector.tensor_scalar(dst[:, t, :], src[:, t, :], mv[:, t, 0:1], rstd[:, t:t + 1],
                                                  ALU.subtract, ALU.mult)
                return ins

            def side_op(g):
                kind = g[0]
                if kind == "v":
                    need_side(dve, g)
                    t0 = g[1] * TPC + 2 * g[2]
                    for t in range(2):
                        ins = nc.vector.tensor_tensor(vals[:, t0 + t, :, 0:HD],
                                                      bank(g)[:, t * D:(t + 1) * D].rearrange("p (h d) -> p h d", h=H),
                                                      bv_b[:, :].rearrange("p (h d) -> p h d", h=H), ALU.add)
                    ins.then_inc(side_v, 1)
                elif kind == "w":
                    need_side(dve, g)
                    if g[1] < 2:
                        dst, n = (w1T, w2T)[g[1]][:, g[2], :], FH
                        nc.vector.tensor_scalar(dst, bank(g).bitcast(BF16)[:, 0:n], -1.0, None, ALU.add)\
                            .then_inc(side_v, 1)
                    else:
                        a = 3 * g[2]
                        full = 3 if g[2] == 0 else 2
                        src = bank(g).bitcast(BF16)[:, 0:3 * D].rearrange("p (t n) -> p t n", t=3)
                        ins = nc.vector.tensor_scalar(w3T[:, a:a + full, :], src[:, 0:full, :], -1.0, None, ALU.add)
                        if full == 2:
                            r = FROWS[FT - 1]
                            ins = nc.vector.tensor_scalar(w3T[0:r, FT - 1, :], src[0:r, 2, :], -1.0, None, ALU.add)
                        ins.then_inc(side_v, 1)
                elif kind == "wo":
                    need_side(dve, g)
                    if g[2] == 0:
                        dve.wait_ge(xb_ok, TPC * (g[1] + 1))
                    t0 = 2 * g[2]
                    rows = x1_of(g[1])
                    nc.vector.tensor_tensor(rows[:, t0:t0 + 2, :], bank(g).rearrange("p (t n) -> p t n", t=2),
                                            rows[:, t0:t0 + 2, :], ALU.add).then_inc(side_v, 1)
                    need_empty(dve, g)
                    variances(rows, t0, t0 + 2)
                    if g[1] == NCH - 1:
                        var_eps(t0, t0 + 2)
                    elif g[2] == 1:
                        var_eps()
                elif kind == "ctxT":
                    need_side(dve, g)
                    src = bank(g).rearrange("p (x r) -> p x r", r=32)
                    link(nc.vector.reciprocal(rd[:, :], src[:, :, HD]))
                    for t in range(TPC):
                        by_head = rd[:, t * G:(t + 1) * G].rearrange("p (h o) -> p h o", o=1)
                        ins = nc.vector.tensor_tensor(ctx_n[:, t, P - G * HD:P].rearrange("p (h d) -> p h d", h=G),
                                                      src[:, t * G:(t + 1) * G, 0:HD],
                                                      by_head.to_broadcast([P, G, HD]), ALU.mult)
                    ins.then_inc(side_v, 1)
                elif kind == "x2T":
                    dve.wait_ge(half_a, half_no[g] + 1)
                    nc.vector.tensor_tensor(x2T_of(g)[:, 1, :, :], bank(g).rearrange("p (k n) -> p k n", k=KT),
                                            x2T_of(g)[:, 0, :, :].bitcast(F32), ALU.subtract).then_inc(side_v, 1)
                elif kind == "up":
                    i, m, rows = up_no[g], g[3], FROWS[g[3]]
                    dve.wait_ge(half_a, half_no[g] + 1)
                    if i >= 2:
                        dve.wait_ge(lo_ok, i - 1)
                    nc.vector.scalar_tensor_tensor(out=hid[0:rows, i % 2, :], in0=th[0:rows, i % 2, :], scalar=1.0,
                                                   in1=bank(g)[0:rows, HALF:CH], op0=ALU.add, op1=ALU.mult)\
                        .then_inc(side_v, 1)
                    need_empty(dve, g)
                    if m == 0 and i >= FT and g[1:3] != (NCH - 1, 1):
                        prev = ups[i - 1]
                        need_side(dve, ("down", prev[1], prev[2]))
                    nc.vector.tensor_copy(hT_of(g)[0:rows, 0, m, :], hid[0:rows, i % 2, :]).then_inc(hid_ok, 1)
                elif kind == "down":
                    need_side(dve, g)
                    n = 2 * g[1] + g[2]
                    if n:
                        dve.wait_ge(out_done, 16 * n)
                    nc.vector.scalar_tensor_tensor(out=fin, in0=bank(g).rearrange("p (t n) -> p t n", t=2), scalar=0.5,
                                                   in1=x1_of(g[1])[:, 2 * g[2]:2 * g[2] + 2, :],
                                                   op0=ALU.mult, op1=ALU.add).then_inc(side_v, 1)

            def lo_part(g):
                i, m, rows = up_no[g], g[3], FROWS[g[3]]
                dve.wait_ge(hid_ok, i + 1)
                dve.wait_ge(lo_ok, i)
                nc.vector.tensor_tensor(hT_of(g)[0:rows, 1, m, :], hid[0:rows, i % 2, :],
                                        hT_of(g)[0:rows, 0, m, :].bitcast(F32), ALU.subtract).then_inc(lo_ok, 1)

            def max_turn(u, k):
                i, h, t = turn_of(u, k)
                x = ("turn", u, k)
                bank = max_bank(x)
                if k == 0 and u >= 2:
                    dve.wait_ge(nm_ok, u - 1)
                dve.wait_ge(max_ready, use_no[x] + 1)
                dst = pm[:, u % 2, h * TPC + t, i:i + 1]
                if i < units[u][0]:
                    nc.vector.tensor_reduce(dst, bank, AX.X, ALU.max).then_inc(max_free, 1)
                else:
                    sc = bank[:, 0:(t + 1) * P]
                    nc.vector.tensor_tensor_reduce(out=sc, in0=sc, in1=mask[:, CH - (t + 1) * P:CH], scale=1.0,
                                                   scalar=NEG, op0=ALU.add, op1=ALU.max, accum_out=dst)\
                        .then_inc(max_free, 1)

            def negate(u):
                dve.wait_ge(max_free, turns_to[use_no[("turn", u, n_turns(u) - 1)] + 1])
                if u >= 1:
                    dve.wait_ge(max_ready, use_no[("swap", u - 1)] + 1)
                nc.vector.tensor_reduce(nm[:, :], pm[:, u % 2, :, 0:units[u][0] + 1], AX.X, ALU.max, negate=True)\
                    .then_inc(nm_ok, 1)

            def split_max(u):
                x = ("swap", u)
                dve.wait_ge(max_ready, use_no[x] + 1)
                if u >= 1:
                    dve.wait_ge(m_in, 32 * u)
                m = max_bank(x)[0:G * TPC, 0:P]
                link(nc.vector.tensor_copy(mT[:, 0, :].bitcast(F32R), m))
                nc.vector.tensor_tensor(mT[:, 1, :].bitcast(F32R), m, mT[:, 0, :], ALU.subtract).then_inc(mT_ok, 1)

            def invert(c):
                dve.wait_ge(den_in, 16 * (c + 1))
                n = den_rows(c)
                nc.vector.reciprocal(dens[0:n, :], dens[0:n, :]).then_inc(rden_ok, 1)

            def norm_ctx(c):
                dve.wait_ge(ctx_in, 16 * 2 * KT * (c + 1))
                if c < NCH - 1:
                    nc.vector.tensor_tensor(ctx_c, ctx_c, den_c, ALU.mult).then_inc(ctx_ok, 1)
                else:
                    n = P - G * HD
                    nc.vector.tensor_tensor(ctx_c[:, 0:KT - 1, :], ctx_c[:, 0:KT - 1, :], den_c[:, 0:KT - 1, :],
                                            ALU.mult)
                    nc.vector.tensor_tensor(ctx_c[0:n, KT - 1, :], ctx_c[0:n, KT - 1, :], den_c[0:n, KT - 1, :],
                                            ALU.mult).then_inc(ctx_ok, 1)

            dve.wait_ge(al_in, 16)
            link(nc.vector.tensor_copy(al[:, 1, :].bitcast(F32R), al[:, 0, :]))
            link(nc.vector.tensor_tensor(al[:, 2, :].bitcast(F32R), al[:, 0, :], al[:, 1, :], ALU.subtract))
            dve.wait_ge(x_in, 16)
            variances(xin, 0, TPC)
            var_eps()
            normalise(xin, xin, 1).then_inc(xn_ok, 1)
            nc.vector.memset(pO[:, :], 0.0)
            nc.vector.memset(vals[:, 0:T // P // 2, :, HD:VW], 1.0).then_inc(rows_ok, 1)
            dve.wait_ge(w_in, 128)
            need_side(dve, ("xT", 0, KT - 1))
            dve.wait_ge(x_in, 32)
            variances(xin, 0, TPC)
            var_eps()
            normalise(xin, xin, 2).then_inc(xn_ok, 1)
            for g in head_groups:
                if g[0] == "v":
                    side_op(g)
            for k in range(n_turns(0)):
                max_turn(0, k)
            negate(0)
            split_max(0)
            g = ("gamma",)
            need_side(dve, g)
            link(nc.vector.tensor_scalar(thr[:, 1, 0:3], bank(g)[:, 0:3], 1.0 / (FH * D), QEPS, ALU.mult, ALU.add))
            link(nc.vector.tensor_scalar(thr[:, 0, 0:3], thr[:, 1, 0:3], 0.5, None, ALU.mult))
            nc.vector.tensor_scalar(thr[:, 1, 0:3], thr[:, 0, 0:3], -1.0, None, ALU.mult).then_inc(side_v, 1)
            need_empty(dve, g)
            rstds = 2
            for s, (u, j) in enumerate(steps):
                c = units[u][0]
                ph = s - phase0[c]
                for use in step_turns[s]:
                    max_turn(*use)
                if step_swap[s]:
                    split_max(step_swap[s])
                if s in TERN_STEPS:
                    n, i = s // 2, (2, 0, 1)[s // 2]
                    if s % 2 == 0:
                        if n == 1:
                            dve.wait_ge(tern_ok, 1)
                        nc.vector.tensor_scalar(tern_v[i], w_rows[i], thr[:, 0, i:i + 1], None, ALU.is_gt)\
                            .then_inc(gt_ok, 1)
                    else:
                        dve.wait_ge(gt_ok, n + 1)
                        nc.vector.scalar_tensor_tensor(out=tern_v[i], in0=w_rows[i], scalar=thr[:, 1, i:i + 1],
                                                       in1=tern_v[i], op0=ALU.is_ge, op1=ALU.add).then_inc(tern_ok, 1)
                if s == TERN_STEPS[-1] + 1:
                    dve.wait_ge(tern_ok, 3)
                    nc.vector.memset(vals[:, T // P // 2:T // P, :, HD:VW], 1.0).then_inc(gt_ok, 1)
                if side[s]:
                    side_op(side[s])
                if ph == 4 and c >= 1:
                    invert(c - 1)
                if ph == 7 and c >= 1:
                    norm_ctx(c - 1)
                if c >= 1 and ph == POST_AT[c] + 3:
                    rstds += 1
                    normalise(xn2, x1, rstds).then_inc(xn2_ok, 1)
                if ph == LN_AT[c]:
                    dve.wait_ge(x_in, 16 * (c + 3))
                    variances(xin, 0, TPC)
                    var_eps()
                if ph == LN_AT[c] + 2:
                    rstds += 1
                    normalise(xin, xin, rstds).then_inc(xn_ok, 1)
                if u == NU - 1 and j == 5:
                    invert(c)
                if u == NU - 1 and j == 6:
                    link(nc.vector.memset(ctx_n[:, :, 0:P - G * HD], 0.0))
                if u == NU - 1 and j == 10:
                    norm_ctx(c)
                if s + 1 < NS and step_swap[s + 1]:
                    negate(step_swap[s + 1])
            for g in tail_groups:
                side_op(g)
                if g[0] == "wo":
                    rstds += 1
                    normalise(xn2, x1_of(g[1]), rstds, 2 * g[2], 2 * g[2] + 2).then_inc(xn2_ok, 1)
                if g[0] == "up":
                    lo_part(g)


_INS = ["L0_attn_x", "L0_attn_Wq", "L0_attn_bq", "L0_attn_Wk", "L0_attn_bk", "L0_attn_Wv", "L0_attn_bv",
        "L0_attn_Wo", "L0_attn_bo", "L0_ffn_w1", "L0_ffn_w2", "L0_ffn_w3"]


def _alibi_table(heads, tokens):
    import numpy as np
    ratio = np.float32(2.0 ** (-8.0 / heads))
    slopes = ratio ** np.arange(1, heads + 1, dtype=np.float32)
    distances = np.arange(1 - tokens, 1, dtype=np.float32)
    return (slopes[:, None] * distances[None, :]).astype(np.float32).reshape(128, -1)


def kernel(**inputs):
    import numpy as _np
    import concourse.bacc as _bacc
    from concourse import mybir as _mybir
    from concourse.bass_utils import run_bass_kernel_spmd as _run

    nc = _bacc.Bacc("TRN2", target_bir_lowering=False, num_devices=1)
    arrays, args = {}, []
    for name in _INS:
        a = _np.ascontiguousarray(inputs[name])
        arrays[f"in_{name}"] = a
        args.append(nc.dram_tensor(f"in_{name}", a.shape, _mybir.dt.from_np(a.dtype), kind="ExternalInput").ap())
    table = _alibi_table(16, inputs["L0_attn_x"].shape[1])
    arrays["alibi"] = table
    args.append(nc.dram_tensor("alibi", table.shape, _mybir.dt.float32, kind="ExternalInput").ap())
    shape = inputs["L0_attn_x"].shape
    args.append(nc.dram_tensor("out_0", shape, _mybir.dt.float32, kind="ExternalOutput").ap())
    preln_layer(nc, *args)
    r = _run(nc, [arrays], core_ids=[0])
    return r.results[0]["out_0"]
```
